# Optimizing a Trainium2 kernel written in Bass

```python
import numpy as np
import jax
import jax.numpy as jnp

def _softmax(x, axis=-1):
    return jax.nn.softmax(x, axis=axis)

def _gelu(x):
    return jax.nn.gelu(x, approximate=True)

def _silu(x):
    return jax.nn.silu(x)

def _sigmoid(x):
    return jax.nn.sigmoid(x)

def _layernorm(x, axis=-1, eps=1e-05):
    m = jnp.mean(x, axis=axis, keepdims=True)
    v = jnp.var(x, axis=axis, keepdims=True)
    return (x - m) / jnp.sqrt(v + eps)

def _scatter_add(tgt, idx, src, axis=0):
    return tgt.at[idx].add(src)

def _segment_sum(src, seg, n):
    return jax.ops.segment_sum(src, seg, n)
kernel_name = 'mk_dlrm_tower_d1_rec_r8_dcca1a'

def setup_inputs(seed: int=0):
    np.random.seed(seed)
    _w = jnp.asarray

    def _rec_inputs():
        import jax
        import jax.numpy as jnp
        _tk = jax.random.key(seed)
        dense_ctx = jax.random.normal(jax.random.fold_in(_tk, 190), (1024, 16), jnp.float32)
        ids = jnp.stack([jax.random.randint(jax.random.fold_in(_tk, 200 + f), (1024,), 0, v, jnp.int32) for f, v in enumerate([12500, 1250, 12500, 125000, 12500, 1250, 1250, 1000, 1000, 1250, 12500, 12500, 125000, 125000, 1250, 12500, 12500, 125000, 1250, 1000, 1000, 125000, 125000, 125000, 125000, 1000, 12500, 125000, 12500, 1250, 125000, 1000])], axis=1)
        tbl_0 = 0.05 * jax.random.normal(jax.random.fold_in(_tk, 500 + 0), (12500, 16), jnp.float32)
        tbl_1 = 0.05 * jax.random.normal(jax.random.fold_in(_tk, 500 + 1), (1250, 16), jnp.float32)
        tbl_2 = 0.05 * jax.random.normal(jax.random.fold_in(_tk, 500 + 2), (12500, 16), jnp.float32)
        tbl_3 = 0.05 * jax.random.normal(jax.random.fold_in(_tk, 500 + 3), (125000, 16), jnp.float32)
        tbl_4 = 0.05 * jax.random.normal(jax.random.fold_in(_tk, 500 + 4), (12500, 16), jnp.float32)
        tbl_5 = 0.05 * jax.random.normal(jax.random.fold_in(_tk, 500 + 5), (1250, 16), jnp.float32)
        tbl_6 = 0.05 * jax.random.normal(jax.random.fold_in(_tk, 500 + 6), (1250, 16), jnp.float32)
        tbl_7 = 0.05 * jax.random.normal(jax.random.fold_in(_tk, 500 + 7), (1000, 16), jnp.float32)
        tbl_8 = 0.05 * jax.random.normal(jax.random.fold_in(_tk, 500 + 8), (1000, 16), jnp.float32)
        tbl_9 = 0.05 * jax.random.normal(jax.random.fold_in(_tk, 500 + 9), (1250, 16), jnp.float32)
        tbl_10 = 0.05 * jax.random.normal(jax.random.fold_in(_tk, 500 + 10), (12500, 16), jnp.float32)
        tbl_11 = 0.05 * jax.random.normal(jax.random.fold_in(_tk, 500 + 11), (12500, 16), jnp.float32)
        tbl_12 = 0.05 * jax.random.normal(jax.random.fold_in(_tk, 500 + 12), (125000, 16), jnp.float32)
        tbl_13 = 0.05 * jax.random.normal(jax.random.fold_in(_tk, 500 + 13), (125000, 16), jnp.float32)
        tbl_14 = 0.05 * jax.random.normal(jax.random.fold_in(_tk, 500 + 14), (1250, 16), jnp.float32)
        tbl_15 = 0.05 * jax.random.normal(jax.random.fold_in(_tk, 500 + 15), (12500, 16), jnp.float32)
        tbl_16 = 0.05 * jax.random.normal(jax.random.fold_in(_tk, 500 + 16), (12500, 16), jnp.float32)
        tbl_17 = 0.05 * jax.random.normal(jax.random.fold_in(_tk, 500 + 17), (125000, 16), jnp.float32)
        tbl_18 = 0.05 * jax.random.normal(jax.random.fold_in(_tk, 500 + 18), (1250, 16), jnp.float32)
        tbl_19 = 0.05 * jax.random.normal(jax.random.fold_in(_tk, 500 + 19), (1000, 16), jnp.float32)
        tbl_20 = 0.05 * jax.random.normal(jax.random.fold_in(_tk, 500 + 20), (1000, 16), jnp.float32)
        tbl_21 = 0.05 * jax.random.normal(jax.random.fold_in(_tk, 500 + 21), (125000, 16), jnp.float32)
        tbl_22 = 0.05 * jax.random.normal(jax.random.fold_in(_tk, 500 + 22), (125000, 16), jnp.float32)
        tbl_23 = 0.05 * jax.random.normal(jax.random.fold_in(_tk, 500 + 23), (125000, 16), jnp.float32)
        tbl_24 = 0.05 * jax.random.normal(jax.random.fold_in(_tk, 500 + 24), (125000, 16), jnp.float32)
        tbl_25 = 0.05 * jax.random.normal(jax.random.fold_in(_tk, 500 + 25), (1000, 16), jnp.float32)
        tbl_26 = 0.05 * jax.random.normal(jax.random.fold_in(_tk, 500 + 26), (12500, 16), jnp.float32)
        tbl_27 = 0.05 * jax.random.normal(jax.random.fold_in(_tk, 500 + 27), (125000, 16), jnp.float32)
        tbl_28 = 0.05 * jax.random.normal(jax.random.fold_in(_tk, 500 + 28), (12500, 16), jnp.float32)
        tbl_29 = 0.05 * jax.random.normal(jax.random.fold_in(_tk, 500 + 29), (1250, 16), jnp.float32)
        tbl_30 = 0.05 * jax.random.normal(jax.random.fold_in(_tk, 500 + 30), (125000, 16), jnp.float32)
        tbl_31 = 0.05 * jax.random.normal(jax.random.fold_in(_tk, 500 + 31), (1000, 16), jnp.float32)
        _rk = jax.random.fold_in(_tk, 7)
        W_top1 = 0.0693375 * jax.random.normal(jax.random.fold_in(_tk, 801), (208, 512), jnp.float32)
        W_top2 = 0.0441942 * jax.random.normal(jax.random.fold_in(_tk, 802), (512, 256), jnp.float32)
        W_top3 = 0.0625 * jax.random.normal(jax.random.fold_in(_tk, 803), (256, 1), jnp.float32)
        b_top1 = jnp.zeros((512,), jnp.float32)
        b_top2 = jnp.zeros((256,), jnp.float32)
        return (dense_ctx, ids, tbl_0, tbl_1, tbl_2, tbl_3, tbl_4, tbl_5, tbl_6, tbl_7, tbl_8, tbl_9, tbl_10, tbl_11, tbl_12, tbl_13, tbl_14, tbl_15, tbl_16, tbl_17, tbl_18, tbl_19, tbl_20, tbl_21, tbl_22, tbl_23, tbl_24, tbl_25, tbl_26, tbl_27, tbl_28, tbl_29, tbl_30, tbl_31, W_top1, b_top1, W_top2, b_top2, W_top3)
    dense_ctx, ids, tbl_0, tbl_1, tbl_2, tbl_3, tbl_4, tbl_5, tbl_6, tbl_7, tbl_8, tbl_9, tbl_10, tbl_11, tbl_12, tbl_13, tbl_14, tbl_15, tbl_16, tbl_17, tbl_18, tbl_19, tbl_20, tbl_21, tbl_22, tbl_23, tbl_24, tbl_25, tbl_26, tbl_27, tbl_28, tbl_29, tbl_30, tbl_31, W_top1, b_top1, W_top2, b_top2, W_top3 = _rec_inputs()

    def _L0_rec_setup():
        import jax, jax.numpy as jnp
        import numpy as np
        B, M, D = (2048, 32, 16)
        LAYERS = [64, 64, 64]
        key = jax.random.key(seed)
        ks = jax.random.split(key, 4)
        inp = {'embeddings': jax.random.normal(ks[0], (B, M, D), dtype=jnp.float32)}
        hk_1 = M
        for i, hk in enumerate(LAYERS):
            scale = (2.0 / (M * hk_1 + hk)) ** 0.5
            inp[f'W{i}'] = jax.random.normal(ks[i + 1], (M, hk_1, hk), dtype=jnp.float32) * scale
            hk_1 = hk
        return inp
    _L0_rec_all = _L0_rec_setup()
    _L0_rec_in = {k: v for k, v in _L0_rec_all.items() if k in ('W0', 'W1', 'W2')}
    del _L0_rec_all
    return {'dense_ctx': dense_ctx, 'ids': ids, 'tbl_0': tbl_0, 'tbl_1': tbl_1, 'tbl_2': tbl_2, 'tbl_3': tbl_3, 'tbl_4': tbl_4, 'tbl_5': tbl_5, 'tbl_6': tbl_6, 'tbl_7': tbl_7, 'tbl_8': tbl_8, 'tbl_9': tbl_9, 'tbl_10': tbl_10, 'tbl_11': tbl_11, 'tbl_12': tbl_12, 'tbl_13': tbl_13, 'tbl_14': tbl_14, 'tbl_15': tbl_15, 'tbl_16': tbl_16, 'tbl_17': tbl_17, 'tbl_18': tbl_18, 'tbl_19': tbl_19, 'tbl_20': tbl_20, 'tbl_21': tbl_21, 'tbl_22': tbl_22, 'tbl_23': tbl_23, 'tbl_24': tbl_24, 'tbl_25': tbl_25, 'tbl_26': tbl_26, 'tbl_27': tbl_27, 'tbl_28': tbl_28, 'tbl_29': tbl_29, 'tbl_30': tbl_30, 'tbl_31': tbl_31, 'W_top1': W_top1, 'b_top1': b_top1, 'W_top2': W_top2, 'b_top2': b_top2, 'W_top3': W_top3, 'L0_rec_W0': _L0_rec_in['W0'], 'L0_rec_W1': _L0_rec_in['W1'], 'L0_rec_W2': _L0_rec_in['W2']}

def reference(dense_ctx, ids, tbl_0, tbl_1, tbl_2, tbl_3, tbl_4, tbl_5, tbl_6, tbl_7, tbl_8, tbl_9, tbl_10, tbl_11, tbl_12, tbl_13, tbl_14, tbl_15, tbl_16, tbl_17, tbl_18, tbl_19, tbl_20, tbl_21, tbl_22, tbl_23, tbl_24, tbl_25, tbl_26, tbl_27, tbl_28, tbl_29, tbl_30, tbl_31, W_top1, b_top1, W_top2, b_top2, W_top3, L0_rec_W0, L0_rec_W1, L0_rec_W2):
    import jax
    import jax.numpy as jnp

    def _L0_rec_ref(embeddings, W0, W1, W2):
        import jax, jax.numpy as jnp
        import numpy as np
        B, M, D = (2048, 32, 16)
        LAYERS = [64, 64, 64]
        x0 = embeddings
        xk = x0
        outs = []
        for W in (W0, W1, W2):
            xk = jax.nn.relu(jnp.einsum('bmd,bhd,mhk->bkd', x0, xk, W))
            outs.append(jnp.sum(xk, axis=2))
        return jnp.concatenate(outs, axis=1)
    e = jnp.stack([tbl_0[ids[:, 0]], tbl_1[ids[:, 1]], tbl_2[ids[:, 2]], tbl_3[ids[:, 3]], tbl_4[ids[:, 4]], tbl_5[ids[:, 5]], tbl_6[ids[:, 6]], tbl_7[ids[:, 7]], tbl_8[ids[:, 8]], tbl_9[ids[:, 9]], tbl_10[ids[:, 10]], tbl_11[ids[:, 11]], tbl_12[ids[:, 12]], tbl_13[ids[:, 13]], tbl_14[ids[:, 14]], tbl_15[ids[:, 15]], tbl_16[ids[:, 16]], tbl_17[ids[:, 17]], tbl_18[ids[:, 18]], tbl_19[ids[:, 19]], tbl_20[ids[:, 20]], tbl_21[ids[:, 21]], tbl_22[ids[:, 22]], tbl_23[ids[:, 23]], tbl_24[ids[:, 24]], tbl_25[ids[:, 25]], tbl_26[ids[:, 26]], tbl_27[ids[:, 27]], tbl_28[ids[:, 28]], tbl_29[ids[:, 29]], tbl_30[ids[:, 30]], tbl_31[ids[:, 31]]], axis=1)
    z = _L0_rec_ref(e, L0_rec_W0, L0_rec_W1, L0_rec_W2)
    z = z.reshape(z.shape[0], -1)
    h = jnp.concatenate([z, dense_ctx], axis=1)
    h = jnp.maximum(h @ W_top1 + b_top1, 0.0)
    h = jnp.maximum(h @ W_top2 + b_top2, 0.0)
    y = h @ W_top3
    return y

_drawn_inputs = setup_inputs


def setup_inputs(seed=0):
    import zlib

    import numpy as np

    out = dict(_drawn_inputs(seed))
    spreads = {'b_top1': (0.0, 2.0), 'b_top2': (0.0, 0.8)}
    factors = {'tbl_0': 8.0,
     'tbl_1': 8.0,
     'tbl_2': 8.0,
     'tbl_3': 8.0,
     'tbl_4': 8.0,
     'tbl_5': 8.0,
     'tbl_6': 8.0,
     'tbl_7': 8.0,
     'tbl_8': 8.0,
     'tbl_9': 8.0,
     'tbl_10': 8.0,
     'tbl_11': 8.0,
     'tbl_12': 8.0,
     'tbl_13': 8.0,
     'tbl_14': 8.0,
     'tbl_15': 8.0,
     'tbl_16': 8.0,
     'tbl_17': 8.0,
     'tbl_18': 8.0,
     'tbl_19': 8.0,
     'tbl_20': 8.0,
     'tbl_21': 8.0,
     'tbl_22': 8.0,
     'tbl_23': 8.0,
     'tbl_24': 8.0,
     'tbl_25': 8.0,
     'tbl_26': 8.0,
     'tbl_27': 8.0,
     'tbl_28': 8.0,
     'tbl_29': 8.0,
     'tbl_30': 8.0,
     'tbl_31': 8.0,
     'L0_rec_W0': 3.626,
     'L0_rec_W1': 8.0,
     'L0_rec_W2': 8.0,
     'dense_ctx': 7.609}
    for name, (base, spread) in spreads.items():
        noise = np.random.default_rng([zlib.crc32(name.encode()), seed]).standard_normal(out[name].shape)
        drawn = base * np.exp(spread * noise) if base else spread * noise
        out[name] = jnp.asarray(drawn.astype(out[name].dtype))
    for name, factor in factors.items():
        out[name] = (out[name] * factor).astype(out[name].dtype)
    return out
```

```python
from contextlib import ExitStack

import concourse.bass as bass
from concourse import mybir

F32 = mybir.dt.float32
I32 = mybir.dt.int32
ALU = mybir.AluOpType
ACT = mybir.ActivationFunctionType
AX_X = mybir.AxisListType.X

P = 128
BATCH = 1024
FIELDS = 32
DIM = 16
MAPS = 64
DENSE = 16
HID1, HID2 = 512, 256
ROWS = [12500, 1250, 12500, 125000, 12500, 1250, 1250, 1000, 1000, 1250, 12500, 12500, 125000, 125000, 1250,
        12500, 12500, 125000, 1250, 1000, 1000, 125000, 125000, 125000, 125000, 1000, 12500, 125000, 12500,
        1250, 125000, 1000]

COLS = BATCH * DIM
HALF = 512
PAIR = 2 * HALF
STEPS = COLS // PAIR
STEP_B = BATCH // STEPS
HALF_B = STEP_B // 2
QUART = P // FIELDS
GATHERS = STEP_B // QUART
GROUP = 2
TILES = FIELDS * MAPS // P
GROUPS = TILES // GROUP
SHIFT_TILES = 4
SHIFT_GROUPS = SHIFT_TILES // GROUP
SCRATCH_ROWS = FIELDS + FIELDS // 2
RING = 3
PER_STEP = 2 * GROUPS + SHIFT_GROUPS
X0_LOADS = 16 * QUART * (1 + SHIFT_TILES)


def first(s):
    return isinstance(s, int) and s == 0


def cin_tower_kernel(nc, table, ids, id_offset, dense_t, w0_a, w0_b, w0_sq, w1, w2,
                     wt1_a, wt1_b, bt1, wt2, bt2, wt3, x0_rows, out):
    with ExitStack() as ctx:
        def sb(name, shape, dt=F32):
            return ctx.enter_context(nc.sbuf_tensor(name, shape, dt))

        def bank(name):
            return ctx.enter_context(nc.psum_tensor(name, [P, HALF], F32))

        def sem(name):
            return ctx.enter_context(nc.semaphore(name))

        ids_sb = sb("ids_sb", [P, BATCH // QUART], I32)
        off_sb = sb("off_sb", [P, GATHERS], I32)
        row_sb = sb("row_sb", [P, 2, GATHERS], I32)
        emb = sb("emb", [P, 2, GATHERS * DIM])
        w0a_sb = sb("w0a_sb", [P, SHIFT_TILES, MAPS])
        w0b_sb = sb("w0b_sb", [P, SHIFT_TILES, MAPS])
        w0s_sb = sb("w0s_sb", [P, SHIFT_TILES, MAPS])
        wsq_in = sb("wsq_in", [P, MAPS])
        wsq_sb = sb("wsq_sb", [P, MAPS])
        w1_sb = sb("w1_sb", [P, TILES, MAPS])
        w2_sb = sb("w2_sb", [P, TILES, MAPS])
        x0x4 = sb("x0x4", [P, PAIR])
        x0sh = sb("x0sh", [P, SHIFT_TILES, PAIR])
        x0bc = sb("x0bc", [P, TILES, PAIR])
        prod = sb("prod", [P, RING, GROUP, PAIR])
        squares = sb("squares", [P, PAIR])
        x1 = sb("x1", [P, PAIR])
        x2 = sb("x2", [P, PAIR])
        relu = sb("relu", [P, 3, HALF])
        z = sb("z", [P, 3, STEPS * HALF_B])
        zt_a = sb("zt_a", [P, BATCH])
        zt_b = sb("zt_b", [MAPS + DENSE, BATCH])
        wt1a_sb = sb("wt1a_sb", [P, HID1])
        wt1b_sb = sb("wt1b_sb", [MAPS + DENSE, HID1])
        wt2_sb = sb("wt2_sb", [P, HID1 // P, HID2])
        wt3_sb = sb("wt3_sb", [P, HID2 // P])
        bt1_sb = sb("bt1_sb", [P, HID1 // P])
        bt2_sb = sb("bt2_sb", [P, HID2 // P])
        h1 = x0bc[:, 0:2, :].rearrange("p a (b n) -> p (a b) n", b=2)
        h2 = x0bc[:, 2:3, :].rearrange("p a (b n) -> p (a b) n", b=2)
        y_sb = sb("y_sb", [1, BATCH])

        y0_ps, y1_ps, y2_ps = bank("y0_ps"), bank("y1_ps"), bank("y2_ps")
        mlp_ps = [bank(f"mlp_ps{i}") for i in range(4)]

        ids_in = sem("ids_in")
        weights_in = sem("weights_in")
        mlp_in = sem("mlp_in")
        gathered = [sem(f"gathered{i}") for i in range(2)]
        scratch_out = [sem(f"scratch_out{i}") for i in range(2)]
        x0_in = sem("x0_in")
        bc_in = [sem(f"bc_in{g}") for g in range(GROUPS)]
        w0_ready = sem("w0_ready")
        products = sem("products")
        products_used = sem("products_used")
        squared = sem("squared")
        squares_used = sem("squares_used")
        relu_done = [sem(f"relu{l}_done") for l in range(3)]
        spread_done = [sem(f"spread{l}_done") for l in range(2)]
        summed = [sem(f"summed{l}") for l in range(3)]
        zt_ready = sem("zt_ready")
        mlp_mm = sem("mlp_mm")
        mlp_act = sem("mlp_act")
        stored = sem("stored")

        def layer0_end(s):
            return SHIFT_GROUPS if first(s) else s * PER_STEP - (GROUPS - SHIFT_GROUPS)

        def layer1_end(s):
            return PER_STEP * s + SHIFT_GROUPS + GROUPS

        def layer2_end(s, last=False):
            return PER_STEP * s + SHIFT_GROUPS + PER_STEP - (SHIFT_GROUPS if last else 0)

        assert PER_STEP % RING == 0

        def slot0(s):
            return 0 if first(s) else (SHIFT_GROUPS + GROUPS) % RING

        SLOT1 = SHIFT_GROUPS % RING

        def slot2(last=False):
            return (SHIFT_GROUPS + GROUPS + (0 if last else SHIFT_GROUPS)) % RING

        block = ctx.enter_context(nc.Block())

        def cols(s):
            return bass.ds(s * PAIR, PAIR)

        @block.sync
        def _(sp):
            sp.dma_start(ids_sb[:], ids).then_inc(ids_in, 16)
            sp.dma_start(off_sb[:], id_offset).then_inc(ids_in, 16)
            for dst, src in ((w0a_sb, w0_a), (w0b_sb, w0_b), (wsq_in, w0_sq), (w1_sb, w1), (w2_sb, w2)):
                sp.dma_start(dst[:], src).then_inc(weights_in, 16)
            for dst, src in ((wt1a_sb[:], wt1_a), (wt1b_sb[:], wt1_b), (wt2_sb[:], wt2), (wt3_sb[:], wt3),
                             (bt1_sb[:], bt1), (bt2_sb[:], bt2), (zt_b[MAPS:, :], dense_t)):
                sp.dma_start(dst, src).then_inc(mlp_in, 16)

            def store_scratch(s, turn, n):
                sp.wait_ge(gathered[turn], n * 16 * GATHERS)
                sp.dma_start(x0_rows[0:FIELDS, cols(s)].rearrange("f (q c) -> f q c", q=QUART),
                             emb[:, turn, :]).then_inc(scratch_out[turn], 16)
                sp.dma_start(x0_rows[FIELDS:SCRATCH_ROWS, cols(s)].rearrange("f (q c) -> f q c", q=QUART),
                             emb[0:QUART * (SCRATCH_ROWS - FIELDS), turn, :]).then_inc(scratch_out[turn], 16)

            def load_x0(s):
                for g in range(QUART):
                    part = slice(FIELDS * g, FIELDS * (g + 1))
                    sp.dma_start(x0x4[part, :], x0_rows[0:FIELDS, cols(s)]).then_inc(x0_in, 16)
                    for t in range(SHIFT_TILES):
                        shift = QUART * t + g + 1
                        sp.dma_start(x0sh[part, t, :],
                                     x0_rows[shift:shift + FIELDS, cols(s)]).then_inc(x0_in, 16)

            def load_broadcast(s, g):
                view = x0_rows[0:FIELDS, cols(s)].rearrange("(g t h) c -> g h t c", t=GROUP, h=2)
                for h in range(2):
                    sp.dma_start(x0bc[MAPS * h:MAPS * (h + 1), GROUP * g:GROUP * (g + 1), :],
                                 view[g, h].unsqueeze(0).to_broadcast([MAPS, GROUP, PAIR])).then_inc(bc_in[g], 16)

            def step(s, turn, n):
                sp.wait_ge(scratch_out[turn], n * 32)
                sp.wait_ge(products_used, layer0_end(s))
                load_x0(s + 1)
                for g in range(GROUPS):
                    sp.wait_ge(products, layer2_end(s) - GROUPS + g + 1)
                    load_broadcast(s + 1, g)

            store_scratch(0, 0, 1)
            sp.wait_ge(scratch_out[0], 32)
            load_x0(0)
            for g in range(GROUPS):
                load_broadcast(0, g)
            store_scratch(1, 1, 1)
            store_scratch(2, 0, 2)
            step(0, 1, 1)
            with sp.Fori(0, (STEPS - 4) // 2) as i:
                store_scratch(i * 2 + 3, 1, i + 2)
                step(i * 2 + 1, 0, i + 2)
                store_scratch(i * 2 + 4, 0, i + 3)
                step(i * 2 + 2, 1, i + 2)
            store_scratch(STEPS - 1, 1, STEPS // 2)
            step(STEPS - 3, 0, STEPS // 2)
            step(STEPS - 2, 1, STEPS // 2)
            sp.wait_ge(mlp_act, 2 * (HID1 // P + HID2 // P + 1))
            sp.dma_start(out.rearrange("b o -> o b"), y_sb[:]).then_inc(stored, 16)
            sp.wait_ge(stored, 16)

        @block.gpsimd
        def _(pool):
            pool.wait_ge(ids_in, 32)

            def gather(s, turn, n, reuse=True):
                if reuse:
                    pool.wait_ge(scratch_out[turn], n * 32)
                pool.tensor_tensor(row_sb[:, turn, :], ids_sb[:, bass.ds(s * GATHERS, GATHERS)], off_sb[:],
                                   ALU.add)
                pool.drain()
                for n in range(GATHERS):
                    pool.indirect_dma_start(emb[:, turn, DIM * n:DIM * (n + 1)], None, table,
                                            bass.IndirectOffsetOnAxis(row_sb[:, turn, n:n + 1], 0)
                                            ).then_inc(gathered[turn], 16)

            def square(s):
                pool.wait_ge(x0_in, X0_LOADS * (s + 1))
                if not first(s):
                    pool.wait_ge(squares_used, s)
                pool.tensor_tensor(squares[:], x0x4[:], x0x4[:], ALU.mult).then_inc(squared, 1)

            gather(0, 0, 0, reuse=False)
            gather(1, 1, 0, reuse=False)
            square(0)
            gather(2, 0, 1)
            square(1)
            gather(3, 1, 1)
            with pool.Fori(1, STEPS // 2 - 1) as i:
                square(i * 2)
                gather(i * 2 + 2, 0, i + 1)
                square(i * 2 + 1)
                gather(i * 2 + 3, 1, i + 1)
            square(STEPS - 2)
            square(STEPS - 1)

        @block.vector
        def _(dve):
            dve.wait_ge(weights_in, 16 * 5)
            dve.tensor_tensor(w0s_sb[:], w0a_sb[:], w0b_sb[:], ALU.add).then_inc(w0_ready, 1)
            dve.tensor_scalar(wsq_sb[:], wsq_in[:], 1.0 / QUART, None, ALU.mult).then_inc(w0_ready, 1)
            dve.wait_ge(w0_ready, 1)
            own = slice(P - FIELDS, P)
            dve.tensor_copy(w0s_sb[own, SHIFT_TILES - 1, :], w0a_sb[own, SHIFT_TILES - 1, :]).then_inc(w0_ready, 1)

            def product(end, slot, left, right, fresh=False):
                if not fresh:
                    dve.wait_ge(products_used, end - RING)
                dve.tensor_tensor(prod[:, slot, :, :], left,
                                  right.unsqueeze(1).to_broadcast([P, GROUP, PAIR]), ALU.mult).then_inc(products, 1)

            def layer0(s):
                dve.wait_ge(x0_in, X0_LOADS * (s + 1))
                for g in range(SHIFT_GROUPS):
                    end = layer0_end(s) - SHIFT_GROUPS + g + 1
                    product(end, (slot0(s) + g) % RING, x0sh[:, GROUP * g:GROUP * (g + 1), :], x0x4[:], first(s))

            def layer(s, l, x, slot, end):
                dve.wait_ge(spread_done[l - 1], 4 * (s + 1))
                for g in range(GROUPS):
                    if l == 1:
                        dve.wait_ge(bc_in[g], 32 * (s + 1))
                    product(end - GROUPS + g + 1, (slot + g) % RING, x0bc[:, GROUP * g:GROUP * (g + 1), :], x[:],
                            first(s) and l == 1 and SHIFT_GROUPS + g < RING)

            def sums(s, l):
                dve.wait_ge(relu_done[l], s + 1)
                dve.tensor_reduce(z[:, l, bass.ds(s * HALF_B, HALF_B)],
                                  relu[:, l, :].rearrange("p (b d) -> p b d", d=DIM), AX_X,
                                  ALU.add).then_inc(summed[l], 1)

            def step(s, last=False):
                layer(s, 1, x1, SLOT1, layer1_end(s))
                sums(s, 0)
                if not first(s):
                    sums(s - 1, 2)
                if not last:
                    layer0(s + 1)
                layer(s, 2, x2, slot2(last), layer2_end(s, last))
                sums(s, 1)

            layer0(0)
            step(0)
            with dve.Fori(1, STEPS - 1) as s:
                step(s)
            step(STEPS - 1, last=True)
            sums(STEPS - 1, 2)
            for l in range(3):
                dve.wait_ge(summed[l], STEPS)
            for l, dst in enumerate((zt_a[0:MAPS, :], zt_a[MAPS:P, :], zt_b[0:MAPS, :])):
                halves = dst.rearrange("p (s h b) -> p s h b", h=2, b=HALF_B)
                for h in range(2):
                    dve.tensor_copy(halves[:, :, h, :],
                                    z[MAPS * h:MAPS * (h + 1), l, :].rearrange("p (s b) -> p s b", b=HALF_B)
                                    ).then_inc(zt_ready, 1)

        @block.scalar
        def _(act):
            def finish(s, l, ps, x=None, x_read=None):
                if x is not None:
                    if x_read is not None:
                        act.wait_ge(products, x_read)
                    for h in range(2):
                        for copy in range(2):
                            act.activation(x[MAPS * copy:MAPS * (copy + 1), HALF * h:HALF * (h + 1)],
                                           ps[MAPS * h:MAPS * (h + 1), :], ACT.Relu).then_inc(spread_done[l], 1)
                if not first(s):
                    act.wait_ge(summed[l], s)
                act.activation(relu[:, l, :], ps[:], ACT.Relu).then_inc(relu_done[l], 1)

            def step(s, last=False):
                act.wait_ge(products_used, layer1_end(s))
                finish(s, 1, y1_ps, x2, None if first(s) else layer2_end(s - 1))
                if not last:
                    act.wait_ge(products_used, layer0_end(s + 1))
                    finish(s + 1, 0, y0_ps, x1, layer1_end(s))
                act.wait_ge(products_used, layer2_end(s, last))
                finish(s, 2, y2_ps)

            act.wait_ge(products_used, layer0_end(0))
            finish(0, 0, y0_ps, x1)
            step(0)
            with act.Fori(1, STEPS - 1) as s:
                step(s)
            step(STEPS - 1, last=True)
            act.wait_ge(mlp_in, 16 * 7)
            n = 0
            for c in range(2):
                for j in range(HID1 // P):
                    n += 1
                    act.wait_ge(mlp_mm, n)
                    act.activation(h1[:, j, :], mlp_ps[(n - 1) % 4][:], ACT.Relu,
                                   bias=bt1_sb[:, j:j + 1]).then_inc(mlp_act, 1)
                for j in range(HID2 // P):
                    n += 1
                    act.wait_ge(mlp_mm, n)
                    act.activation(h2[:, j, :], mlp_ps[(n - 1) % 4][:], ACT.Relu,
                                   bias=bt2_sb[:, j:j + 1]).then_inc(mlp_act, 1)
                n += 1
                act.wait_ge(mlp_mm, n)
                act.activation(y_sb[:, HALF * c:HALF * (c + 1)], mlp_ps[(n - 1) % 4][0:1, :],
                               ACT.Copy).then_inc(mlp_act, 1)

        @block.tensor
        def _(pe):
            def contract(ps, w, moving, first, final):
                for h in range(2):
                    last = pe.matmul(ps[MAPS * h:MAPS * (h + 1), :], w, moving[:, HALF * h:HALF * (h + 1)],
                                     start=first, stop=final)
                return last

            def groups(end, slot, count, ps, w, start):
                for g in range(count):
                    pe.wait_ge(products, end - count + g + 1)
                    for t in range(GROUP):
                        last = contract(ps, w[:, GROUP * g + t, :], prod[:, (slot + g) % RING, t, :],
                                        start and g == 0 and t == 0, g == count - 1 and t == GROUP - 1)
                    last.then_inc(products_used, 1)

            def layer0(s):
                if not first(s):
                    pe.wait_ge(spread_done[0], 4 * s)
                    pe.wait_ge(relu_done[0], s)
                pe.wait_ge(squared, s + 1)
                contract(y0_ps, wsq_sb[:], squares[:], True, False).then_inc(squares_used, 1)
                groups(layer0_end(s), slot0(s), SHIFT_GROUPS, y0_ps, w0s_sb, False)

            def layer(s, l, ps, w, slot, end):
                if not first(s):
                    if l == 1:
                        pe.wait_ge(spread_done[1], 4 * s)
                    pe.wait_ge(relu_done[l], s)
                groups(end, slot, GROUPS, ps, w, True)

            def step(s, last=False):
                layer(s, 1, y1_ps, w1_sb, SLOT1, layer1_end(s))
                if not last:
                    layer0(s + 1)
                layer(s, 2, y2_ps, w2_sb, slot2(last), layer2_end(s, last))

            pe.wait_ge(w0_ready, 3)
            pe.wait_ge(weights_in, 16 * 5)
            layer0(0)
            step(0)
            with pe.Fori(1, STEPS - 1) as s:
                step(s)
            step(STEPS - 1, last=True)

            pe.wait_ge(zt_ready, 6)
            pe.wait_ge(mlp_in, 16 * 7)
            n = 0

            def target():
                if n >= 4:
                    pe.wait_ge(mlp_act, n - 3)
                return mlp_ps[n % 4]

            for c in range(2):
                b = slice(HALF * c, HALF * (c + 1))
                for j in range(HID1 // P):
                    ps = target()
                    out_f = slice(P * j, P * (j + 1))
                    pe.matmul(ps[:], wt1a_sb[:, out_f], zt_a[:, b], start=True, stop=False)
                    pe.matmul(ps[:], wt1b_sb[:, out_f], zt_b[:, b], start=False, stop=True).then_inc(mlp_mm, 1)
                    n += 1
                for j in range(HID2 // P):
                    ps = target()
                    pe.wait_ge(mlp_act, n - j)
                    for k in range(HID1 // P):
                        last = pe.matmul(ps[:], wt2_sb[:, k, P * j:P * (j + 1)], h1[:, k, :], start=k == 0,
                                         stop=k == HID1 // P - 1)
                    last.then_inc(mlp_mm, 1)
                    n += 1
                ps = target()
                pe.wait_ge(mlp_act, n)
                for k in range(HID2 // P):
                    last = pe.matmul(ps[0:1, :], wt3_sb[:, k:k + 1], h2[:, k, :], start=k == 0,
                                     stop=k == HID2 // P - 1)
                last.then_inc(mlp_mm, 1)
                n += 1


def kernel(**inputs):
    import numpy as np
    import concourse.bacc as bacc
    from concourse.bass_utils import run_bass_kernel_spmd

    get = {k: np.asarray(v) for k, v in inputs.items()}
    w0 = get["L0_rec_W0"]
    m = np.arange(FIELDS)
    shift = QUART * np.arange(SHIFT_TILES)[None, None, :] + np.arange(QUART)[:, None, None] + 1
    other = (m[None, :, None] + shift) % FIELDS
    own = np.broadcast_to(m[None, :, None], other.shape)
    offsets = np.concatenate([[0], np.cumsum(ROWS)[:-1]]).astype(np.int32)

    def rows_of(w):
        return w.reshape(TILES, P, MAPS).transpose(1, 0, 2)

    arrays = {
        "table": np.concatenate([get[f"tbl_{f}"] for f in range(FIELDS)], axis=0),
        "ids": get["ids"].T.reshape(FIELDS, STEPS, QUART, GATHERS).transpose(0, 2, 1, 3).reshape(P, -1),
        "id_offset": np.repeat(offsets, QUART)[:, None].repeat(GATHERS, axis=1),
        "dense_t": get["dense_ctx"].T,
        "w0_a": w0[own, other].reshape(P, SHIFT_TILES, MAPS),
        "w0_b": w0[other, own].reshape(P, SHIFT_TILES, MAPS),
        "w0_sq": np.tile(w0[m, m], (QUART, 1)),
        "w1": rows_of(get["L0_rec_W1"]),
        "w2": rows_of(get["L0_rec_W2"]),
        "wt1_a": get["W_top1"][0:P],
        "wt1_b": get["W_top1"][P:],
        "bt1": get["b_top1"].reshape(HID1 // P, P).T,
        "wt2": get["W_top2"].reshape(HID1 // P, P, HID2).transpose(1, 0, 2),
        "bt2": get["b_top2"].reshape(HID2 // P, P).T,
        "wt3": get["W_top3"].reshape(HID2 // P, P).T,
    }
    arrays = {k: np.ascontiguousarray(a) for k, a in arrays.items()}
    nc = bacc.Bacc("TRN2", target_bir_lowering=False, num_devices=1)
    args = [nc.dram_tensor(k, a.shape, mybir.dt.from_np(a.dtype), kind="ExternalInput").ap()
            for k, a in arrays.items()]
    x0_rows = nc.dram_tensor("x0_rows", [SCRATCH_ROWS, COLS], F32, kind="Internal").ap()
    out = nc.dram_tensor("out", [BATCH, 1], F32, kind="ExternalOutput").ap()
    cin_tower_kernel(nc, *args, x0_rows, out)
    r = run_bass_kernel_spmd(nc, [arrays], core_ids=[0])
    return r.results[0]["out"]
```

```python
from contextlib import ExitStack

import concourse.bass as bass
from concourse import mybir

F32 = mybir.dt.float32
F32R = mybir.dt.float32r
I32 = mybir.dt.int32
ALU = mybir.AluOpType
ACT = mybir.ActivationFunctionType
AX_X = mybir.AxisListType.X

P = 128
BATCH = 1024
FIELDS = 32
DIM = 16
MAPS = 64
DENSE = 16
HID1, HID2 = 512, 256
ROWS = [12500, 1250, 12500, 125000, 12500, 1250, 1250, 1000, 1000, 1250, 12500, 12500, 125000, 125000, 1250,
        12500, 12500, 125000, 1250, 1000, 1000, 125000, 125000, 125000, 125000, 1000, 12500, 125000, 12500,
        1250, 125000, 1000]

COLS = BATCH * DIM
HALF = 512
PAIR = 2 * HALF
STEPS = COLS // PAIR
STEP_B = BATCH // STEPS
HALF_B = STEP_B // 2
QUART = P // FIELDS
GATHERS = STEP_B // QUART
GROUP = 2
TILES = FIELDS * MAPS // P
POOL_TILES = 3
GROUPS = -(-(TILES - POOL_TILES) // GROUP)
TWICE = 4
TWICE_GROUPS = TWICE // GROUP
GROUP_TILES = [range(GROUP * g, min(GROUP * (g + 1), TILES - POOL_TILES)) for g in range(GROUPS)]
POOL_RANGE = range(TILES - POOL_TILES, TILES)
SHIFT_TILES = 4
SHIFT_GROUPS = SHIFT_TILES // GROUP
SHIFT_RANGES = [range(GROUP * g, GROUP * (g + 1)) for g in range(SHIFT_GROUPS)]
LOW_BEFORE = 3
SHIFT_BEHIND = 5
X0_BEFORE = 2
POOL_BEFORE = 5
EARLY_GATHERS = 11
FIRST_GATHERS = 8
BEFORE_SQUARES = 10
FIRST_BANKS = 4
BANKS = 2 * SHIFT_TILES
RING = 4
PER_STEP = 2 * GROUPS + SHIFT_GROUPS
X0_LOADS = 16 * QUART


def first(s):
    return isinstance(s, int) and s == 0


def cin_tower_kernel(nc, table, ids, id_offset, dense_t, w0_a, w0_b, w0_sq, w1, w2, shifts,
                     wt1_a, wt1_b, bt1, wt2, bt2, wt3, x0_rows, x0_parts, out):
    with ExitStack() as ctx:
        def sb(name, shape, dt=F32):
            return ctx.enter_context(nc.sbuf_tensor(name, shape, dt))

        def bank(name):
            return ctx.enter_context(nc.psum_tensor(name, [P, HALF], F32))

        def sem(name):
            return ctx.enter_context(nc.semaphore(name))

        ids_sb = sb("ids_sb", [P, BATCH // QUART], I32)
        off_sb = sb("off_sb", [P, GATHERS], I32)
        row_first = sb("row_first", [P, 3, GATHERS], I32)
        row_sb = sb("row_sb", [P, 2, GATHERS], I32)
        emb = sb("emb", [P, 2, GATHERS * DIM])
        emb_hi = sb("emb_hi", [P, 2, GATHERS * DIM], F32R)
        emb_lo = sb("emb_lo", [P, 2, GATHERS * DIM], F32R)
        shifts_sb = sb("shifts_sb", [2 * FIELDS, SHIFT_TILES, P], F32R)
        x0hl = sb("x0hl", [2 * FIELDS, PAIR], F32R)
        w0s_sb = sb("w0s_sb", [P, SHIFT_TILES, MAPS])
        wsq_sb = sb("wsq_sb", [P, MAPS])
        w1_sb = sb("w1_sb", [P, TILES, MAPS])
        w2_sb = sb("w2_sb", [P, TILES, MAPS])
        x0x4 = sb("x0x4", [P, PAIR])
        x0sh = sb("x0sh", [P, SHIFT_TILES, PAIR])
        x0bc = sb("x0bc", [P, TILES + TWICE + POOL_TILES, PAIR])
        prod = sb("prod", [P, RING, GROUP, PAIR])
        squares = sb("squares", [P, PAIR])
        pool_prod = sb("pool_prod", [P, POOL_TILES, PAIR])
        shifts_in = pool_prod[0:2 * FIELDS, 0, 0:SHIFT_TILES * P].rearrange("p (t c) -> p t c", c=P)
        w0a_sb = pool_prod[:, 1, 0:SHIFT_TILES * MAPS].rearrange("p (t k) -> p t k", k=MAPS)
        w0b_sb = pool_prod[:, 1, SHIFT_TILES * MAPS:2 * SHIFT_TILES * MAPS].rearrange("p (t k) -> p t k", k=MAPS)
        wsq_in = pool_prod[:, 2, 0:MAPS]
        x1_sb = sb("x1_sb", [P, 2, HALF])
        x2_sb = sb("x2_sb", [P, 2, HALF])
        relu = sb("relu", [P, 3, HALF])
        z = sb("z", [P, 3, STEPS * HALF_B])
        zt_a = x0bc[:, 3, :]
        zt_b = x0bc[0:MAPS + DENSE, 0, :]
        wt1a_sb = x0bc[:, 1, 0:HID1]
        wt1b_sb = x0bc[0:MAPS + DENSE, 1, HID1:2 * HID1]
        wt2_sb = x0bc[:, 2, :].rearrange("p (k n) -> p k n", n=HID2)
        wt3_sb = sb("wt3_sb", [P, HID2 // P])
        bt1_sb = sb("bt1_sb", [P, HID1 // P])
        bt2_sb = sb("bt2_sb", [P, HID2 // P])
        h1 = x0bc[:, 5:7, :].rearrange("p a (b n) -> p (a b) n", b=2)
        h2 = x0bc[:, 7:8, :].rearrange("p a (b n) -> p (a b) n", b=2)
        y_sb = x0bc[0:1, 4, :]

        y0_ps, y1_ps, y2_ps = bank("y0_ps"), bank("y1_ps"), bank("y2_ps")
        shift_ps = bank("shift_ps")
        x1_ps = ctx.enter_context(nc.psum_tensor("x1_ps", [P, 2, HALF], F32))
        x2_ps = ctx.enter_context(nc.psum_tensor("x2_ps", [P, 2, HALF], F32))
        mlp_ps = [x1_ps[:, 0, :], x1_ps[:, 1, :], x2_ps[:, 0, :], x2_ps[:, 1, :]]

        ids_in = sem("ids_in")
        weights_in = sem("weights_in")
        mlp_in = sem("mlp_in")
        gathered = [sem(f"gathered{i}") for i in range(2)]
        scratch_out = [sem(f"scratch_out{i}") for i in range(2)]
        x0_in = sem("x0_in")
        x0hl_in = sem("x0hl_in")
        high_done = sem("high_done")
        low_done = sem("low_done")
        shifted = sem("shifted")
        shift_copied = sem("shift_copied")
        bc_in = [sem(f"bc_in{g}") for g in range(GROUPS)]
        bc_pool_in = sem("bc_pool_in")
        w0_ready = sem("w0_ready")
        products = sem("products")
        products_used = sem("products_used")
        pool_products = sem("pool_products")
        pool_products_used = sem("pool_products_used")
        x0_placed = sem("x0_placed")
        squared = sem("squared")
        squares_used = sem("squares_used")
        relu_done = [sem(f"relu{l}_done") for l in range(3)]
        spread_done = [sem(f"spread{l}_done") for l in range(2)]
        copied = [sem(f"copied{l}") for l in range(2)]
        summed = [sem(f"summed{l}") for l in range(3)]
        zt_ready = sem("zt_ready")
        mlp_mm = sem("mlp_mm")
        mlp_act = sem("mlp_act")
        stored = sem("stored")

        def layer0_end(s):
            return SHIFT_GROUPS if first(s) else s * PER_STEP - (GROUPS - SHIFT_GROUPS)

        def layer1_end(s):
            return PER_STEP * s + SHIFT_GROUPS + GROUPS

        def layer2_end(s, last=False):
            return PER_STEP * s + SHIFT_GROUPS + PER_STEP - (SHIFT_GROUPS if last else 0)

        def place(turn, t):
            if turn == 1 and t < TWICE:
                return TILES + t
            if turn == 1 and t >= POOL_RANGE[0]:
                return TILES + TWICE + t - POOL_RANGE[0]
            return t

        assert PER_STEP % RING == 0

        def slot0(s):
            return 0 if first(s) else (SHIFT_GROUPS + GROUPS) % RING

        SLOT1 = SHIFT_GROUPS % RING

        def slot2(last=False):
            return (SHIFT_GROUPS + GROUPS + (0 if last else SHIFT_GROUPS)) % RING

        def shift_bank(s, k):
            return [shift_ps[:], y1_ps[:], y2_ps[:], x2_ps[:, 0, :]][k % FIRST_BANKS] if first(s) else shift_ps[:]

        block = ctx.enter_context(nc.Block())

        def cols(s):
            return bass.ds(s * PAIR, PAIR)

        @block.sync
        def _(sp):
            sp.dma_start(ids_sb[:], ids).then_inc(ids_in, 16)
            sp.dma_start(off_sb[:], id_offset).then_inc(ids_in, 16)
            for dst, src in ((w0a_sb, w0_a), (w0b_sb, w0_b), (wsq_in, w0_sq), (w1_sb[:], w1), (w2_sb[:], w2),
                             (shifts_in, shifts)):
                sp.dma_start(dst, src).then_inc(weights_in, 16)

            def store_scratch(s, turn):
                sp.wait_ge(low_done, s + 1)
                for rows, part in ((x0_rows[:, cols(s)], emb[:]), (x0_parts[0:FIELDS, cols(s)], emb_hi[:]),
                                   (x0_parts[FIELDS:2 * FIELDS, cols(s)], emb_lo[:])):
                    sp.dma_start(rows.rearrange("f (q c) -> f q c", q=QUART),
                                 part.bitcast(F32)[:, turn, :]).then_inc(scratch_out[turn], 16)

            def load_parts(s, turn, n):
                if not first(s):
                    sp.wait_ge(shifted, s * BANKS)
                sp.wait_ge(scratch_out[turn], n * 48)
                sp.dma_start(x0hl[:].bitcast(F32), x0_parts[:, cols(s)]).then_inc(x0hl_in, 16)

            def load_x0(s):
                for g in range(QUART):
                    sp.dma_start(x0x4[FIELDS * g:FIELDS * (g + 1), :], x0_rows[:, cols(s)]).then_inc(x0_in, 16)

            def load_broadcast(s, turn, tiles, arrived):
                view = x0_rows[:, cols(s)].rearrange("(t h) c -> h t c", h=2)
                a, b = tiles[0], tiles[-1] + 1
                to = place(turn, a)
                for h in range(2):
                    sp.dma_start(x0bc[MAPS * h:MAPS * (h + 1), to:to + b - a, :],
                                 view[h, a:b].unsqueeze(0).to_broadcast([MAPS, b - a, PAIR])).then_inc(arrived, 16)

            def step(s, turn, n=None):
                if not first(s):
                    sp.wait_ge(products, layer2_end(s - 1))
                for g in range(TWICE_GROUPS):
                    load_broadcast(s + 1, 1 - turn, GROUP_TILES[g], bc_in[g])
                if not first(s):
                    sp.wait_ge(pool_products, s * 2)
                load_broadcast(s + 1, 1 - turn, POOL_RANGE, bc_pool_in)
                if n is not None and not first(s):
                    store_scratch(s + 2, turn)
                    load_parts(s + 2, turn, n)
                for g in range(TWICE_GROUPS, GROUPS):
                    if g == X0_BEFORE and n is not None and not first(s):
                        sp.wait_ge(products_used, layer0_end(s + 1))
                        load_x0(s + 2)
                    sp.wait_ge(products, layer2_end(s) - GROUPS + g + 1)
                    load_broadcast(s + 1, 1 - turn, GROUP_TILES[g], bc_in[g])
                if first(s):
                    store_scratch(2, 0)
                    load_parts(2, 0, n)
                    sp.wait_ge(products_used, layer0_end(1))
                    load_x0(2)

            store_scratch(0, 0)
            load_parts(0, 0, 1)
            load_x0(0)
            for g in range(GROUPS):
                if g == 3:
                    sp.wait_ge(gathered[1], 16 * GATHERS)
                load_broadcast(0, 0, GROUP_TILES[g], bc_in[g])
                if g == 0:
                    load_broadcast(0, 0, POOL_RANGE, bc_pool_in)
                if g == 3:
                    store_scratch(1, 1)
                if g == 4:
                    load_parts(1, 1, 1)
            sp.wait_ge(products_used, layer0_end(0))
            load_x0(1)
            step(0, 0, 2)
            with sp.Fori(0, (STEPS - 4) // 2) as i:
                step(i * 2 + 1, 1, i + 2)
                step(i * 2 + 2, 0, i + 3)
            step(STEPS - 3, 1, STEPS // 2)
            step(STEPS - 2, 0)
            sp.wait_ge(products, layer2_end(STEPS - 2))
            for dst, src in ((wt1a_sb, wt1_a), (wt1b_sb, wt1_b), (wt2_sb, wt2), (wt3_sb[:], wt3),
                             (bt1_sb[:], bt1), (bt2_sb[:], bt2), (zt_b[MAPS:, :], dense_t)):
                sp.dma_start(dst, src).then_inc(mlp_in, 16)
            sp.wait_ge(mlp_act, 2 * (HID1 // P + HID2 // P + 1))
            sp.dma_start(out.rearrange("b o -> o b"), y_sb).then_inc(stored, 16)
            sp.wait_ge(stored, 16)

        @block.gpsimd
        def _(pool):
            pool.wait_ge(ids_in, 32)

            def rows(s, turn, n):
                pool.wait_ge(scratch_out[turn], n * 48)
                pool.tensor_tensor(row_sb[:, turn, :], ids_sb[:, bass.ds(s * GATHERS, GATHERS)], off_sb[:], ALU.add)
                pool.drain()

            def gather(turn, row, part):
                for n in range(GATHERS)[part]:
                    pool.indirect_dma_start(emb[:, turn, DIM * n:DIM * (n + 1)], None, table,
                                            bass.IndirectOffsetOnAxis(row[:, n:n + 1], 0)
                                            ).then_inc(gathered[turn], 16)

            def square(s):
                pool.wait_ge(x0_in, X0_LOADS * (s + 1))
                if not first(s):
                    pool.wait_ge(squares_used, s)
                pool.tensor_tensor(squares[:], x0x4[:], x0x4[:], ALU.mult).then_inc(squared, 1)

            def layer(s, turn, l, x):
                pool.wait_ge(copied[l - 1], 4 * (s + 1))
                if l == 1:
                    pool.wait_ge(bc_pool_in, 32 * (s + 1))
                if not (first(s) and l == 1):
                    pool.wait_ge(pool_products_used, s * 2 + l - 1)
                at = place(turn, POOL_RANGE[0])
                pool.tensor_tensor(pool_prod[:], x0bc[:, at:at + POOL_TILES, :],
                                   x[:].rearrange("p h c -> p (h c)").unsqueeze(1).to_broadcast([P, POOL_TILES, PAIR]),
                                   ALU.mult).then_inc(pool_products, 1)

            def step(s, turn, n=None):
                layer(s, turn, 1, x1_sb)
                if first(s):
                    pool.wait_ge(scratch_out[0], 48)
                    gather(0, row_first[:, 2], slice(0, FIRST_GATHERS))
                if not (isinstance(s, int) and s == STEPS - 1):
                    square(s + 1)
                row = row_sb[:, 1 - turn]
                if first(s):
                    gather(0, row_first[:, 2], slice(FIRST_GATHERS, None))
                elif n is not None:
                    rows(s + 3, 1 - turn, n)
                    gather(1 - turn, row, slice(0, EARLY_GATHERS))
                layer(s, turn, 2, x2_sb)
                if first(s):
                    rows(3, 1, n)
                    gather(1, row, slice(None))
                elif n is not None:
                    gather(1 - turn, row, slice(EARLY_GATHERS, None))

            pool.tensor_tensor(row_first[:], ids_sb[:, 0:3 * GATHERS].rearrange("p (s n) -> p s n", s=3),
                               off_sb[:].unsqueeze(1).to_broadcast([P, 3, GATHERS]), ALU.add)
            pool.drain()
            gather(0, row_first[:, 0], slice(None))
            gather(1, row_first[:, 1], slice(0, BEFORE_SQUARES))
            square(0)
            gather(1, row_first[:, 1], slice(BEFORE_SQUARES, None))
            pool.wait_ge(w0_ready, 4)
            step(0, 0, 1)
            with pool.Fori(0, (STEPS - 4) // 2) as i:
                step(i * 2 + 1, 1, i + 2)
                step(i * 2 + 2, 0, i + 2)
            for s in range(STEPS - 3, STEPS):
                step(s, s % 2)

        @block.vector
        def _(dve):
            dve.wait_ge(weights_in, 16 * 6)
            dve.tensor_tensor(w0s_sb[:], w0a_sb, w0b_sb, ALU.add).then_inc(w0_ready, 1)
            dve.tensor_scalar(wsq_sb[:], wsq_in, 1.0 / QUART, None, ALU.mult).then_inc(w0_ready, 1)
            dve.wait_ge(w0_ready, 1)
            own = slice(P - FIELDS, P)
            dve.tensor_copy(w0s_sb[own, SHIFT_TILES - 1, :], w0a_sb[own, SHIFT_TILES - 1, :]).then_inc(w0_ready, 1)

            def product(end, slot, count, left, right, fresh=False):
                if not fresh:
                    dve.wait_ge(products_used, end - RING)
                right = right[:].rearrange("p h c -> p (h c)").unsqueeze(1).to_broadcast([P, count, PAIR])
                dve.tensor_tensor(prod[:, slot, 0:count, :], left, right, ALU.mult).then_inc(products, 1)

            def low(s, turn, n):
                dve.wait_ge(high_done, s + 1)
                if not (isinstance(n, int) and n == 1):
                    dve.wait_ge(scratch_out[turn], (n - 1) * 48)
                dve.tensor_tensor(emb_lo[:, turn, :], emb[:, turn, :], emb_hi[:, turn, :].bitcast(F32),
                                  ALU.subtract).then_inc(low_done, 1)

            def layer0(s):
                dve.wait_ge(x0_placed, s + 1)
                for g in range(SHIFT_GROUPS):
                    dve.wait_ge(shift_copied, BANKS * s + 2 * GROUP * (g + 1))
                    end = layer0_end(s) - SHIFT_GROUPS + g + 1
                    product(end, (slot0(s) + g) % RING, GROUP, x0sh[:, GROUP * g:GROUP * (g + 1), :], x1_ps, first(s))

            def layer(s, turn, l, x, slot, end, low_of=None, low_before=LOW_BEFORE):
                dve.wait_ge(spread_done[l - 1], 4 * (s + 1))
                for g in range(GROUPS):
                    if low_of is not None and g == low_before:
                        low(*low_of)
                    if l == 1:
                        dve.wait_ge(bc_in[g], 32 * (s + 1))
                    at, count = place(turn, GROUP_TILES[g][0]), len(GROUP_TILES[g])
                    product(end - GROUPS + g + 1, (slot + g) % RING, count, x0bc[:, at:at + count, :], x,
                            first(s) and l == 1 and SHIFT_GROUPS + g < RING)

            def sums(s, l):
                dve.wait_ge(relu_done[l], s + 1)
                dve.tensor_reduce(z[:, l, bass.ds(s * HALF_B, HALF_B)],
                                  relu[:, l, :].rearrange("p (b d) -> p b d", d=DIM), AX_X,
                                  ALU.add).then_inc(summed[l], 1)

            def step(s, turn, n=None, last=False):
                low_of = None if n is None else (s + 2, turn, n)
                if first(s):
                    layer(0, 0, 1, x1_ps, SLOT1, layer1_end(0), (1, 1, 1), 1)
                else:
                    layer(s, turn, 1, x1_ps, SLOT1, layer1_end(s), low_of)
                sums(s, 0)
                if not first(s):
                    sums(s - 1, 2)
                if not last:
                    layer0(s + 1)
                layer(s, turn, 2, x2_ps, slot2(last), layer2_end(s, last), low_of if first(s) else None)
                sums(s, 1)

            dve.tensor_copy(shifts_sb[:], shifts_in).then_inc(w0_ready, 1)
            low(0, 0, 1)
            layer0(0)
            step(0, 0, 2)
            with dve.Fori(0, (STEPS - 4) // 2) as i:
                step(i * 2 + 1, 1, i + 2)
                step(i * 2 + 2, 0, i + 3)
            step(STEPS - 3, 1, STEPS // 2)
            step(STEPS - 2, 0)
            step(STEPS - 1, 1, last=True)
            sums(STEPS - 1, 2)
            for l in range(3):
                dve.wait_ge(summed[l], STEPS)
            for l, dst in enumerate((zt_a[0:MAPS, :], zt_a[MAPS:P, :], zt_b[0:MAPS, :])):
                halves = dst.rearrange("p (s h b) -> p s h b", h=2, b=HALF_B)
                for h in range(2):
                    dve.tensor_copy(halves[:, :, h, :],
                                    z[MAPS * h:MAPS * (h + 1), l, :].rearrange("p (s b) -> p s b", b=HALF_B)
                                    ).then_inc(zt_ready, 1)

        @block.scalar
        def _(act):
            def high(s, turn, n):
                act.wait_ge(gathered[turn], n * 16 * GATHERS)
                if not (isinstance(n, int) and n == 1):
                    act.wait_ge(scratch_out[turn], (n - 1) * 48)
                act.activation(emb_hi[:, turn, :], emb[:, turn, :], ACT.Copy).then_inc(high_done, 1)

            def copy_shifts(s, part=slice(None)):
                for k in range(BANKS)[part]:
                    act.wait_ge(shifted, BANKS * s + k + 1)
                    act.activation(x0sh[:, k // 2, HALF * (k % 2):HALF * (k % 2 + 1)], shift_bank(s, k),
                                   ACT.Copy).then_inc(shift_copied, 1)

            def place_x0(s):
                act.wait_ge(x0_in, X0_LOADS * (s + 1))
                if not first(s):
                    act.wait_ge(products, layer1_end(s - 1))
                act.activation(x1_ps[:].rearrange("p h c -> p (h c)"), x0x4[:], ACT.Copy).then_inc(x0_placed, 1)

            def finish(s, l, ps, x=None, x_sb=None):
                if x is not None:
                    for to, done in ((x, spread_done[l]), (x_sb, copied[l])):
                        for h in range(2):
                            for copy in range(2):
                                act.activation(to[MAPS * copy:MAPS * (copy + 1), h, :],
                                               ps[MAPS * h:MAPS * (h + 1), :], ACT.Relu).then_inc(done, 1)
                if not first(s):
                    act.wait_ge(summed[l], s)
                act.activation(relu[:, l, :], ps[:], ACT.Relu).then_inc(relu_done[l], 1)

            def step(s, turn=None, n=None, last=False):
                if turn is not None and not first(s):
                    high(s + 2, turn, n)
                if isinstance(s, int) and s < 2:
                    copy_shifts(s + 1)
                if not last:
                    place_x0(s + 1)
                act.wait_ge(products_used, layer1_end(s))
                finish(s, 1, y1_ps, x2_ps, x2_sb)
                if not last:
                    act.wait_ge(products_used, layer0_end(s + 1))
                    finish(s + 1, 0, y0_ps, x1_ps, x1_sb)
                if first(s):
                    high(2, turn, n)
                elif turn is not None:
                    copy_shifts(s + 2)
                act.wait_ge(products_used, layer2_end(s, last))
                finish(s, 2, y2_ps)

            high(0, 0, 1)
            copy_shifts(0, slice(0, BANKS // 2))
            place_x0(0)
            copy_shifts(0, slice(BANKS // 2, None))
            act.wait_ge(products_used, layer0_end(0))
            finish(0, 0, y0_ps, x1_ps, x1_sb)
            high(1, 1, 1)
            step(0, 0, 2)
            step(1, 1, 2)
            with act.Fori(1, (STEPS - 2) // 2) as i:
                step(i * 2, 0, i + 2)
                step(i * 2 + 1, 1, i + 2)
            step(STEPS - 2)
            step(STEPS - 1, last=True)
            act.wait_ge(mlp_in, 16 * 7)
            n = 0
            for c in range(2):
                for j in range(HID1 // P):
                    n += 1
                    act.wait_ge(mlp_mm, n)
                    act.activation(h1[:, j, :], mlp_ps[(n - 1) % 4], ACT.Relu,
                                   bias=bt1_sb[:, j:j + 1]).then_inc(mlp_act, 1)
                for j in range(HID2 // P):
                    n += 1
                    act.wait_ge(mlp_mm, n)
                    act.activation(h2[:, j, :], mlp_ps[(n - 1) % 4], ACT.Relu,
                                   bias=bt2_sb[:, j:j + 1]).then_inc(mlp_act, 1)
                n += 1
                act.wait_ge(mlp_mm, n)
                act.activation(y_sb[:, HALF * c:HALF * (c + 1)], mlp_ps[(n - 1) % 4][0:1, :],
                               ACT.Copy).then_inc(mlp_act, 1)

        @block.tensor
        def _(pe):
            def contract(ps, w, moving, first, final):
                for h in range(2):
                    last = pe.matmul(ps[MAPS * h:MAPS * (h + 1), :], w, moving[:, HALF * h:HALF * (h + 1)],
                                     start=first, stop=final)
                return last

            def shift(s, k):
                if k == 0:
                    pe.wait_ge(x0hl_in, 16 * (s + 1))
                if not first(s):
                    pe.wait_ge(shift_copied, BANKS * s + k)
                elif k >= FIRST_BANKS:
                    pe.wait_ge(shift_copied, k - FIRST_BANKS + 1)
                pe.matmul(shift_bank(s, k), shifts_sb[:, k // 2, :], x0hl[:, HALF * (k % 2):HALF * (k % 2 + 1)],
                          start=True, stop=True).then_inc(shifted, 1)

            def groups(end, slot, tiles, ps, w, start, pool_number=None, shifts_of=None):
                for g, group in enumerate(tiles):
                    if g == POOL_BEFORE:
                        pe.wait_ge(pool_products, pool_number)
                        for t in POOL_RANGE:
                            last = contract(ps, w[:, t, :], pool_prod[:, t - POOL_RANGE[0], :], False, False)
                        last.then_inc(pool_products_used, 1)
                    pe.wait_ge(products, end - len(tiles) + g + 1)
                    for t in group:
                        if shifts_of is not None and 0 <= t - SHIFT_BEHIND < BANKS:
                            shift(shifts_of, t - SHIFT_BEHIND)
                        last = contract(ps, w[:, t, :], prod[:, (slot + g) % RING, t - group[0], :],
                                        start and t == 0, g == len(tiles) - 1 and t == group[-1])
                    last.then_inc(products_used, 1)

            def layer0(s):
                if not first(s):
                    pe.wait_ge(relu_done[0], s)
                pe.wait_ge(squared, s + 1)
                contract(y0_ps, wsq_sb[:], squares[:], True, False).then_inc(squares_used, 1)
                groups(layer0_end(s), slot0(s), SHIFT_RANGES, y0_ps, w0s_sb, False)

            def layer(s, l, ps, w, slot, end, shifts_of=None):
                if not first(s):
                    pe.wait_ge(relu_done[l], s)
                groups(end, slot, GROUP_TILES, ps, w, True, s * 2 + l, shifts_of)

            def step(s, more=True, last=False):
                layer(s, 1, y1_ps, w1_sb, SLOT1, layer1_end(s), s + 1 if isinstance(s, int) and s < 2 else None)
                if not last:
                    layer0(s + 1)
                layer(s, 2, y2_ps, w2_sb, slot2(last), layer2_end(s, last),
                      s + 2 if more and not first(s) else None)

            pe.wait_ge(w0_ready, 4)
            pe.wait_ge(weights_in, 16 * 6)
            for k in range(BANKS):
                shift(0, k)
            layer0(0)
            step(0)
            step(1)
            with pe.Fori(2, STEPS - 2) as s:
                step(s)
            step(STEPS - 2, more=False)
            step(STEPS - 1, more=False, last=True)

            pe.wait_ge(zt_ready, 6)
            pe.wait_ge(mlp_in, 16 * 7)
            n = 0

            def target():
                if n >= 4:
                    pe.wait_ge(mlp_act, n - 3)
                return mlp_ps[n % 4]

            for c in range(2):
                b = slice(HALF * c, HALF * (c + 1))
                for j in range(HID1 // P):
                    ps = target()
                    out_f = slice(P * j, P * (j + 1))
                    pe.matmul(ps, wt1a_sb[:, out_f], zt_a[:, b], start=True, stop=False)
                    pe.matmul(ps, wt1b_sb[:, out_f], zt_b[:, b], start=False, stop=True).then_inc(mlp_mm, 1)
                    n += 1
                for j in range(HID2 // P):
                    ps = target()
                    pe.wait_ge(mlp_act, n - j)
                    for k in range(HID1 // P):
                        last = pe.matmul(ps, wt2_sb[:, k, P * j:P * (j + 1)], h1[:, k, :], start=k == 0,
                                         stop=k == HID1 // P - 1)
                    last.then_inc(mlp_mm, 1)
                    n += 1
                ps = target()
                pe.wait_ge(mlp_act, n)
                for k in range(HID2 // P):
                    last = pe.matmul(ps[0:1, :], wt3_sb[:, k:k + 1], h2[:, k, :], start=k == 0,
                                     stop=k == HID2 // P - 1)
                last.then_inc(mlp_mm, 1)
                n += 1


def kernel(**inputs):
    import numpy as np
    import concourse.bacc as bacc
    from concourse.bass_utils import run_bass_kernel_spmd

    get = {k: np.asarray(v) for k, v in inputs.items()}
    w0 = get["L0_rec_W0"]
    m = np.arange(FIELDS)
    shift = QUART * np.arange(SHIFT_TILES)[None, None, :] + np.arange(QUART)[:, None, None] + 1
    other = (m[None, :, None] + shift) % FIELDS
    own = np.broadcast_to(m[None, :, None], other.shape)
    pick = other.reshape(P, SHIFT_TILES).T[None] == m[:, None, None]
    offsets = np.concatenate([[0], np.cumsum(ROWS)[:-1]]).astype(np.int32)

    def rows_of(w):
        return w.reshape(TILES, P, MAPS).transpose(1, 0, 2)

    arrays = {
        "table": np.concatenate([get[f"tbl_{f}"] for f in range(FIELDS)], axis=0),
        "ids": get["ids"].T.reshape(FIELDS, STEPS, QUART, GATHERS).transpose(0, 2, 1, 3).reshape(P, -1),
        "id_offset": np.repeat(offsets, QUART)[:, None].repeat(GATHERS, axis=1),
        "dense_t": get["dense_ctx"].T,
        "w0_a": w0[own, other].reshape(P, SHIFT_TILES, MAPS),
        "w0_b": w0[other, own].reshape(P, SHIFT_TILES, MAPS),
        "w0_sq": np.tile(w0[m, m], (QUART, 1)),
        "w1": rows_of(get["L0_rec_W1"]),
        "w2": rows_of(get["L0_rec_W2"]),
        "shifts": np.tile(pick.astype(np.float32), (2, 1, 1)),
        "wt1_a": get["W_top1"][0:P],
        "wt1_b": get["W_top1"][P:],
        "bt1": get["b_top1"].reshape(HID1 // P, P).T,
        "wt2": get["W_top2"].reshape(HID1 // P, P, HID2).transpose(1, 0, 2),
        "bt2": get["b_top2"].reshape(HID2 // P, P).T,
        "wt3": get["W_top3"].reshape(HID2 // P, P).T,
    }
    arrays = {k: np.ascontiguousarray(a) for k, a in arrays.items()}
    nc = bacc.Bacc("TRN2", target_bir_lowering=False, num_devices=1)
    args = [nc.dram_tensor(k, a.shape, mybir.dt.from_np(a.dtype), kind="ExternalInput").ap()
            for k, a in arrays.items()]
    x0_rows = nc.dram_tensor("x0_rows", [FIELDS, COLS], F32, kind="Internal").ap()
    x0_parts = nc.dram_tensor("x0_parts", [2 * FIELDS, COLS], F32, kind="Internal").ap()
    out = nc.dram_tensor("out", [BATCH, 1], F32, kind="ExternalOutput").ap()
    cin_tower_kernel(nc, *args, x0_rows, x0_parts, out)
    r = run_bass_kernel_spmd(nc, [arrays], core_ids=[0])
    return r.results[0]["out"]
```

```python
from contextlib import ExitStack

import concourse.bass as bass
from concourse import mybir

F32 = mybir.dt.float32
F32R = mybir.dt.float32r
I32 = mybir.dt.int32
ALU = mybir.AluOpType
ACT = mybir.ActivationFunctionType
AX_X = mybir.AxisListType.X

P = 128
BATCH = 1024
FIELDS = 32
DIM = 16
MAPS = 64
DENSE = 16
HID1, HID2 = 512, 256
ROWS = [12500, 1250, 12500, 125000, 12500, 1250, 1250, 1000, 1000, 1250, 12500, 12500, 125000, 125000, 1250,
        12500, 12500, 125000, 1250, 1000, 1000, 125000, 125000, 125000, 125000, 1000, 12500, 125000, 12500,
        1250, 125000, 1000]

COLS = BATCH * DIM
HALF = 512
PAIR = 2 * HALF
STEPS = COLS // PAIR
STEP_B = BATCH // STEPS
HALF_B = STEP_B // 2
QUART = P // FIELDS
GATHERS = STEP_B // QUART
GROUP = 2
TILES = FIELDS * MAPS // P
POOL_TILES = 3
POOL_RANGES = {1: [13, 14, 15], 2: [13, 14, 15, 12]}
POOL_STEP = len(POOL_RANGES[1]) + len(POOL_RANGES[2])
GROUP_TILES = {1: [range(0, 2), range(2, 4), range(4, 6), range(6, 8), range(8, 10), range(10, 12), range(12, 13)],
               2: [range(0, 2), range(2, 4), range(4, 6), range(6, 8), range(8, 10), range(10, 11), range(11, 12)]}
GROUPS = len(GROUP_TILES[1])
LOADS = GROUP_TILES[1]
TWICE = 4
TWICE_GROUPS = TWICE // GROUP
SHIFTS = [[1, 5, 3, 2], [11, 13, 15, 9], [4, 6, 14, 16]]
SHIFT_TILES = len(SHIFTS)
DISTANCES = [[b - a for a, b in zip(*pair)] for pair in
             [(4 * [0], SHIFTS[0]), (4 * [0], SHIFTS[1]), (4 * [0], SHIFTS[2]), (SHIFTS[0], SHIFTS[1])]]
assert sorted(sum(DISTANCES, [])) == list(range(1, FIELDS // 2 + 1))
OWN_TILE = 2
PAIR_TILES = len(DISTANCES)
SHIFT_GROUPS = PAIR_TILES // GROUP
SHIFT_RANGES = [range(GROUP * g, GROUP * (g + 1)) for g in range(SHIFT_GROUPS)]
LATE = 4
LOW_BEFORE = 5
LATE_LOW_BEFORE = 3
SHIFT_AT = [2, 3, 4, 5, 8, 9]
FIRST_SHIFT_AT = [range(5, 11), range(2, 8)]
SHIFTS_EARLY = 4
X0_BEFORE = 2
POOL_BEFORE = 2
EARLY_GATHERS = 11
FIRST_GATHERS = [(16, 0), (20, 6), (12, 7), (12, 7)]
FIRST_ROWS = len(FIRST_GATHERS) + 3
FIRST_BANKS = 4
BANKS = 2 * SHIFT_TILES
RING = 4
PER_STEP = 2 * GROUPS + SHIFT_GROUPS
X0_LOADS = 16 * QUART
MLP = ([(1, 0, j) for j in range(HID1 // P)] + [(2, 0, j) for j in range(HID2 // P)] +
       [(1, 1, j) for j in range(HID1 // P)] + [(3, 0, 0)] + [(2, 1, j) for j in range(HID2 // P)] + [(3, 1, 0)])
MLP_EARLY = HID1 // P
MLP_BANKS = 4


def first(s):
    return isinstance(s, int) and s == 0


def late(s):
    return isinstance(s, int) and s < LATE


def cin_tower_kernel(nc, table, ids, id_offset, dense_t, w0_a, w0_b, w0_sq, w1, w2, shifts,
                     wt1_a, wt1_b, bt1, wt2, bt2, wt3, x0_rows, x0_parts, out):
    with ExitStack() as ctx:
        def sb(name, shape, dt=F32):
            return ctx.enter_context(nc.sbuf_tensor(name, shape, dt))

        def bank(name):
            return ctx.enter_context(nc.psum_tensor(name, [P, HALF], F32))

        def sem(name):
            return ctx.enter_context(nc.semaphore(name))

        ids_sb = sb("ids_sb", [P, BATCH // QUART], I32)
        off_sb = sb("off_sb", [P, GATHERS], I32)
        row_first = sb("row_first", [P, FIRST_ROWS, GATHERS], I32)
        row_sb = sb("row_sb", [P, 2, GATHERS], I32)
        emb = sb("emb", [P, 2, GATHERS * DIM])
        emb_hi = sb("emb_hi", [P, 2, GATHERS * DIM], F32R)
        emb_lo = sb("emb_lo", [P, 2, GATHERS * DIM], F32R)
        shifts_sb = sb("shifts_sb", [2 * FIELDS, SHIFT_TILES, P], F32R)
        x0hl = sb("x0hl", [2 * FIELDS, PAIR], F32R)
        w0s_sb = sb("w0s_sb", [P, PAIR_TILES, MAPS])
        wsq_sb = sb("wsq_sb", [P, MAPS])
        w1_sb = sb("w1_sb", [P, TILES, MAPS])
        w2_sb = sb("w2_sb", [P, TILES, MAPS])
        x0x4 = sb("x0x4", [P, PAIR])
        x0sh = sb("x0sh", [P, SHIFT_TILES, PAIR])
        x0bc = sb("x0bc", [P, TILES + TWICE + POOL_TILES, PAIR])
        prod = sb("prod", [P, RING, GROUP, PAIR])
        squares = sb("squares", [P, PAIR])
        pool_prod = sb("pool_prod", [P, len(POOL_RANGES[2]), PAIR])
        shifts_in = pool_prod[0:2 * FIELDS, 0, 0:SHIFT_TILES * P].rearrange("p (t c) -> p t c", c=P)
        w0a_sb = pool_prod[:, 1, 0:PAIR_TILES * MAPS].rearrange("p (t k) -> p t k", k=MAPS)
        w0b_sb = pool_prod[:, 1, PAIR_TILES * MAPS:2 * PAIR_TILES * MAPS].rearrange("p (t k) -> p t k", k=MAPS)
        wsq_in = pool_prod[:, 2, 0:MAPS]
        x1_sb = sb("x1_sb", [P, 2, HALF])
        x2_sb = sb("x2_sb", [P, 2, HALF])
        relu = sb("relu", [P, 3, HALF])
        z = sb("z", [P, 3, STEPS * HALF_B])
        zt_a = x0bc[:, 3, :]
        zt_b = x0bc[0:MAPS + DENSE, 0, :]
        wt1a_sb = x0bc[:, 1, 0:HID1]
        wt1b_sb = x0bc[0:MAPS + DENSE, 1, HID1:2 * HID1]
        wt2_sb = x0bc[:, 2, :].rearrange("p (k n) -> p k n", n=HID2)
        wt3_sb = sb("wt3_sb", [P, HID2 // P])
        bt1_sb = sb("bt1_sb", [P, HID1 // P])
        bt2_sb = sb("bt2_sb", [P, HID2 // P])
        h1 = x0bc[:, 13:15, :].rearrange("p a (b n) -> p (a b) n", b=2)
        h2 = x0bc[:, 15:16, :].rearrange("p a (b n) -> p (a b) n", b=2)
        y_sb = x0bc[96:97, 0, :]

        y0_ps, y1_ps, y2_ps = bank("y0_ps"), bank("y1_ps"), bank("y2_ps")
        shift_ps = bank("shift_ps")
        x1_ps = ctx.enter_context(nc.psum_tensor("x1_ps", [P, 2, HALF], F32))
        x2_ps = ctx.enter_context(nc.psum_tensor("x2_ps", [P, 2, HALF], F32))
        mlp_ps = [y0_ps[:], shift_ps[:], x1_ps[:, 0, :], x1_ps[:, 1, :]]

        ids_in = sem("ids_in")
        weights_in = sem("weights_in")
        mlp_in = sem("mlp_in")
        gathered = [sem(f"gathered{i}") for i in range(2)]
        scratch_out = [sem(f"scratch_out{i}") for i in range(2)]
        x0_in = sem("x0_in")
        x0hl_in = sem("x0hl_in")
        high_done = sem("high_done")
        low_done = sem("low_done")
        shifted = sem("shifted")
        shift_copied = sem("shift_copied")
        bc_in = [sem(f"bc_in{g}") for g in range(GROUPS)]
        bc_pool_in = sem("bc_pool_in")
        rows_done = sem("rows_done")
        w0_ready = sem("w0_ready")
        products = sem("products")
        products_used = sem("products_used")
        pool_products = sem("pool_products")
        pool_products_used = sem("pool_products_used")
        x0_placed = sem("x0_placed")
        squared = sem("squared")
        squares_used = sem("squares_used")
        relu_done = [sem(f"relu{l}_done") for l in range(3)]
        spread_done = [sem(f"spread{l}_done") for l in range(2)]
        copied = [sem(f"copied{l}") for l in range(2)]
        summed = [sem(f"summed{l}") for l in range(3)]
        zt_ready = sem("zt_ready")
        mlp_mm = sem("mlp_mm")
        mlp_act = sem("mlp_act")
        stored = sem("stored")

        def layer0_end(s):
            return SHIFT_GROUPS if first(s) else s * PER_STEP - (GROUPS - SHIFT_GROUPS)

        def layer1_end(s):
            return PER_STEP * s + SHIFT_GROUPS + GROUPS

        def layer2_end(s, last=False):
            return PER_STEP * s + SHIFT_GROUPS + PER_STEP - (SHIFT_GROUPS if last else 0)

        def pool_end(s, l):
            return POOL_STEP * s + (POOL_STEP if l == 2 else len(POOL_RANGES[1]))

        def place(turn, t):
            if turn == 1 and t < TWICE:
                return TILES + t
            if turn == 1 and t >= TILES - POOL_TILES:
                return t + TWICE + POOL_TILES
            return t

        assert PER_STEP % RING == 0

        def slot0(s):
            return 0 if first(s) else (SHIFT_GROUPS + GROUPS) % RING

        SLOT1 = SHIFT_GROUPS % RING

        def slot2(last=False):
            return (SHIFT_GROUPS + GROUPS + (0 if last else SHIFT_GROUPS)) % RING

        def shift_bank(s, k):
            return [shift_ps[:], y1_ps[:], y2_ps[:], x2_ps[:, 0, :]][k % FIRST_BANKS] if first(s) else shift_ps[:]

        block = ctx.enter_context(nc.Block())

        def cols(s):
            return bass.ds(s * PAIR, PAIR)

        @block.sync
        def _(sp):
            sp.dma_start(ids_sb[:], ids).then_inc(ids_in, 16)
            sp.dma_start(off_sb[:], id_offset).then_inc(ids_in, 16)
            for dst, src in ((w0a_sb, w0_a), (w0b_sb, w0_b), (wsq_in, w0_sq), (w1_sb[:], w1), (w2_sb[:], w2),
                             (shifts_in, shifts)):
                sp.dma_start(dst, src).then_inc(weights_in, 16)

            def store_scratch(s, turn):
                sp.wait_ge(low_done, s + 1)
                for rows, part in ((x0_rows[:, cols(s)], emb[:]), (x0_parts[0:FIELDS, cols(s)], emb_hi[:]),
                                   (x0_parts[FIELDS:2 * FIELDS, cols(s)], emb_lo[:])):
                    sp.dma_start(rows.rearrange("f (q c) -> f q c", q=QUART),
                                 part.bitcast(F32)[:, turn, :]).then_inc(scratch_out[turn], 16)

            def load_parts(s, turn, n):
                if not first(s):
                    sp.wait_ge(shifted, s * BANKS)
                sp.wait_ge(scratch_out[turn], n * 48)
                sp.dma_start(x0hl[:].bitcast(F32), x0_parts[:, cols(s)]).then_inc(x0hl_in, 16)

            def load_x0(s):
                for g in range(QUART):
                    sp.dma_start(x0x4[FIELDS * g:FIELDS * (g + 1), :], x0_rows[:, cols(s)]).then_inc(x0_in, 16)

            def load_broadcast(s, turn, tiles, arrived):
                view = x0_rows[:, cols(s)].rearrange("(t h) c -> h t c", h=2)
                a, b = tiles[0], tiles[-1] + 1
                to = place(turn, a)
                for h in range(2):
                    sp.dma_start(x0bc[MAPS * h:MAPS * (h + 1), to:to + b - a, :],
                                 view[h, a:b].unsqueeze(0).to_broadcast([MAPS, b - a, PAIR])).then_inc(arrived, 16)

            def step(s, turn, n=None):
                if not first(s):
                    sp.wait_ge(products, layer2_end(s - 1))
                for g in range(TWICE_GROUPS):
                    load_broadcast(s + 1, 1 - turn, LOADS[g], bc_in[g])
                if not first(s):
                    sp.wait_ge(pool_products, pool_end(s - 1, 2))
                load_broadcast(s + 1, 1 - turn, range(TILES - POOL_TILES, TILES), bc_pool_in)
                if n is not None:
                    store_scratch(s + 2, turn)
                    if not late(s):
                        load_parts(s + 2, turn, n)
                for g in range(TWICE_GROUPS, GROUPS):
                    if g == X0_BEFORE + late(s) and n is not None:
                        sp.wait_ge(products_used, layer0_end(s + 1))
                        load_x0(s + 2)
                    if g < GROUPS - 1:
                        after = max(k for k in range(GROUPS) if set(GROUP_TILES[2][k]) & set(LOADS[g]))
                        sp.wait_ge(products, layer2_end(s) - GROUPS + after + 1)
                    else:
                        sp.wait_ge(pool_products, pool_end(s, 2))
                    load_broadcast(s + 1, 1 - turn, LOADS[g], bc_in[g])
                    if late(s) and g == X0_BEFORE:
                        load_parts(s + 2, turn, n)

            store_scratch(0, 0)
            load_parts(0, 0, 1)
            load_x0(0)
            for g in range(GROUPS):
                if g == 3:
                    sp.wait_ge(gathered[1], 16 * GATHERS)
                load_broadcast(0, 0, LOADS[g], bc_in[g])
                if g == 0:
                    load_broadcast(0, 0, range(TILES - POOL_TILES, TILES), bc_pool_in)
                if g == 3:
                    store_scratch(1, 1)
                if g == 4:
                    load_parts(1, 1, 1)
            sp.wait_ge(products_used, layer0_end(0))
            load_x0(1)
            for s in range(LATE):
                step(s, s % 2, s // 2 + 2)
            with sp.Fori(LATE // 2, STEPS // 2 - 1) as i:
                step(i * 2, 0, i + 2)
                step(i * 2 + 1, 1, i + 2)
            step(STEPS - 2, 0)
            sp.wait_ge(products, layer2_end(STEPS - 2))
            for dst, src in ((wt1a_sb, wt1_a), (wt1b_sb, wt1_b), (wt2_sb, wt2), (wt3_sb[:], wt3),
                             (bt1_sb[:], bt1), (bt2_sb[:], bt2), (zt_b[MAPS:, :], dense_t)):
                sp.dma_start(dst, src).then_inc(mlp_in, 16)
            sp.wait_ge(mlp_act, len(MLP))
            sp.dma_start(out.rearrange("b o -> o b"), y_sb).then_inc(stored, 16)
            sp.wait_ge(stored, 16)

        @block.gpsimd
        def _(pool):
            pool.wait_ge(ids_in, 32)

            def rows(s, turn, n):
                pool.wait_ge(scratch_out[turn], n * 48)
                pool.tensor_tensor(row_sb[:, turn, :], ids_sb[:, bass.ds(s * GATHERS, GATHERS)], off_sb[:],
                                   ALU.add).then_inc(rows_done, 1)

            def gather(turn, row, part):
                for n in range(GATHERS)[part]:
                    pool.indirect_dma_start(emb[:, turn, DIM * n:DIM * (n + 1)], None, table,
                                            bass.IndirectOffsetOnAxis(row[:, n:n + 1], 0)
                                            ).then_inc(gathered[turn], 16)

            def layer(s, turn, l, x, rows_of=None):
                if rows_of is not None:
                    pool.wait_ge(rows_done, rows_of - FIRST_ROWS + 1)
                pool.wait_ge(copied[l - 1], 4 * (s + 1))
                if l == 1:
                    pool.wait_ge(bc_pool_in, 32 * (s + 1))
                before = 0 if first(s) and l == 1 else pool_end(s, 1) if l == 2 else pool_end(s - 1, 2)
                for k, t in enumerate(POOL_RANGES[l]):
                    if k < len(POOL_RANGES[3 - l]) and not first(before):
                        pool.wait_ge(pool_products_used, before - len(POOL_RANGES[3 - l]) + k + 1)
                    pool.tensor_tensor(pool_prod[:, k], x0bc[:, place(turn, t), :],
                                       x[:].rearrange("p h c -> p (h c)"), ALU.mult).then_inc(pool_products, 1)

            def first_gathers(a, b):
                for k in range(a, b):
                    s, n = divmod(k, GATHERS)
                    if s >= 2 and n == 0:
                        pool.wait_ge(scratch_out[s % 2], s // 2 * 48)
                    gather(s % 2, row_first[:, s], slice(n, n + 1))

            def step(s, turn, n):
                row = row_sb[:, 1 - turn]
                rows(s + 3, 1 - turn, n)
                layer(s, turn, 1, x1_sb, s + 3)
                gather(1 - turn, row, slice(0, EARLY_GATHERS))
                layer(s, turn, 2, x2_sb)
                gather(1 - turn, row, slice(EARLY_GATHERS, None))

            pool.tensor_tensor(row_first[:], ids_sb[:, 0:FIRST_ROWS * GATHERS].rearrange("p (s n) -> p s n", n=GATHERS),
                               off_sb[:].unsqueeze(1).to_broadcast([P, FIRST_ROWS, GATHERS]), ALU.add)
            pool.drain()
            done = 2 * GATHERS
            first_gathers(0, done)
            pool.wait_ge(w0_ready, 4)
            for s, counts in enumerate(FIRST_GATHERS):
                for l, x in ((1, x1_sb), (2, x2_sb)):
                    layer(s, s % 2, l, x)
                    first_gathers(done, done + counts[l - 1])
                    done += counts[l - 1]
            assert done == (len(FIRST_GATHERS) + 3) * GATHERS
            with pool.Fori(len(FIRST_GATHERS) // 2, STEPS // 2 - 2) as i:
                step(i * 2, 0, i + 1)
                step(i * 2 + 1, 1, i + 2)
            step(STEPS - 4, 0, STEPS // 2 - 1)
            for s in range(STEPS - 3, STEPS):
                layer(s, s % 2, 1, x1_sb)
                layer(s, s % 2, 2, x2_sb)

        @block.vector
        def _(dve):
            dve.wait_ge(weights_in, 16 * 6)
            dve.tensor_tensor(w0s_sb[:], w0a_sb, w0b_sb, ALU.add).then_inc(w0_ready, 1)
            dve.tensor_scalar(wsq_sb[:], wsq_in, 1.0 / QUART, None, ALU.mult).then_inc(w0_ready, 1)
            dve.wait_ge(w0_ready, 1)
            own = slice(P - FIELDS, P)
            dve.tensor_copy(w0s_sb[own, OWN_TILE, :], w0a_sb[own, OWN_TILE, :]).then_inc(w0_ready, 1)

            def product(end, slot, count, left, right, fresh=False):
                if not fresh:
                    dve.wait_ge(products_used, end - RING)
                right = right[:].rearrange("p h c -> p (h c)").unsqueeze(1).to_broadcast([P, count, PAIR])
                dve.tensor_tensor(prod[:, slot, 0:count, :], left, right, ALU.mult).then_inc(products, 1)

            def low(s, turn, n):
                dve.wait_ge(high_done, s + 1)
                if not (isinstance(n, int) and n == 1):
                    dve.wait_ge(scratch_out[turn], (n - 1) * 48)
                dve.tensor_tensor(emb_lo[:, turn, :], emb[:, turn, :], emb_hi[:, turn, :].bitcast(F32),
                                  ALU.subtract).then_inc(low_done, 1)

            def layer0(s):
                dve.wait_ge(x0_placed, s + 1)
                dve.wait_ge(shift_copied, BANKS * s + 4)
                product(layer0_end(s) - 1, slot0(s), GROUP, x0sh[:, 0:GROUP, :], x1_ps, first(s))
                dve.wait_ge(shift_copied, BANKS * s + BANKS)
                if not first(s):
                    dve.wait_ge(products_used, layer0_end(s) - RING)
                slot = (slot0(s) + 1) % RING
                dve.tensor_tensor(prod[:, slot, 0, :], x0sh[:, 2, :], x1_ps[:].rearrange("p h c -> p (h c)"), ALU.mult)
                dve.tensor_tensor(prod[:, slot, 1, :], x0sh[:, 0, :], x0sh[:, 1, :], ALU.mult).then_inc(products, 1)

            def layer(s, turn, l, x, slot, end, low_of=None, low_before=LOW_BEFORE):
                for g in range(GROUPS):
                    if low_of is not None and g == low_before:
                        low(*low_of)
                    if l == 1:
                        dve.wait_ge(bc_in[g], 32 * (s + 1))
                    at, count = place(turn, GROUP_TILES[l][g][0]), len(GROUP_TILES[l][g])
                    fresh = first(s) and l == 1 and SHIFT_GROUPS + g < RING
                    if g == 0:
                        if not fresh:
                            dve.wait_ge(products_used, end - GROUPS + g + 1 - RING)
                        for h in range(2):
                            dve.wait_ge(spread_done[l - 1], 4 * s + 2 * h + 2)
                            half = slice(HALF * h, HALF * (h + 1))
                            last = dve.tensor_tensor(prod[:, slot, 0:count, half], x0bc[:, at:at + count, half],
                                                     x[:, h].unsqueeze(1).to_broadcast([P, count, HALF]), ALU.mult)
                        last.then_inc(products, 1)
                    else:
                        product(end - GROUPS + g + 1, (slot + g) % RING, count, x0bc[:, at:at + count, :], x, fresh)
                if low_of is not None and low_before == GROUPS:
                    low(*low_of)

            def sums(s, l):
                dve.wait_ge(relu_done[l], s + 1)
                dve.tensor_reduce(z[:, l, bass.ds(s * HALF_B, HALF_B)],
                                  relu[:, l, :].rearrange("p (b d) -> p b d", d=DIM), AX_X,
                                  ALU.add).then_inc(summed[l], 1)

            def mlp_input(c):
                steps = STEPS // 2
                for l in range(3):
                    dve.wait_ge(summed[l], steps * (c + 1))
                for l, dst in enumerate((zt_a[0:MAPS, :], zt_a[MAPS:P, :], zt_b[0:MAPS, :])):
                    dst = dst[:, HALF * c:HALF * (c + 1)].rearrange("p (s h b) -> p s h b", h=2, b=HALF_B)
                    for h in range(2):
                        src = z[MAPS * h:MAPS * (h + 1), l, steps * HALF_B * c:steps * HALF_B * (c + 1)]
                        dve.tensor_copy(dst[:, :, h, :],
                                        src.rearrange("p (s b) -> p s b", b=HALF_B)).then_inc(zt_ready, 1)

            def step(s, turn, n=None, last=False):
                low_of = None if n is None else (s + 2, turn, n)
                if first(s):
                    layer(0, 0, 1, x1_ps, SLOT1, layer1_end(0), (1, 1, 1), 1)
                else:
                    layer(s, turn, 1, x1_ps, SLOT1, layer1_end(s), None if late(s) else low_of,
                          GROUPS if isinstance(s, int) and s == LATE else LOW_BEFORE)
                sums(s, 0)
                if not first(s):
                    sums(s - 1, 2)
                if last:
                    mlp_input(0)
                else:
                    layer0(s + 1)
                layer(s, turn, 2, x2_ps, slot2(last), layer2_end(s, last),
                      low_of if late(s) else None, LATE_LOW_BEFORE)
                sums(s, 1)

            dve.tensor_copy(shifts_sb[:], shifts_in).then_inc(w0_ready, 1)
            low(0, 0, 1)
            layer0(0)
            for s in range(LATE + 2):
                step(s, s % 2, s // 2 + 2)
            with dve.Fori(LATE // 2 + 1, STEPS // 2 - 1) as i:
                step(i * 2, 0, i + 2)
                step(i * 2 + 1, 1, i + 2)
            step(STEPS - 2, 0)
            step(STEPS - 1, 1, last=True)
            sums(STEPS - 1, 2)
            mlp_input(1)

        @block.scalar
        def _(act):
            def high(s, turn, n):
                act.wait_ge(gathered[turn], n * 16 * GATHERS)
                if not (isinstance(n, int) and n == 1):
                    act.wait_ge(scratch_out[turn], (n - 1) * 48)
                act.activation(emb_hi[:, turn, :], emb[:, turn, :], ACT.Copy).then_inc(high_done, 1)

            def copy_shifts(s, part=slice(None)):
                for k in range(BANKS)[part]:
                    act.wait_ge(shifted, BANKS * s + k + 1)
                    act.activation(x0sh[:, k // 2, HALF * (k % 2):HALF * (k % 2 + 1)], shift_bank(s, k),
                                   ACT.Copy).then_inc(shift_copied, 1)

            def square(s):
                act.wait_ge(x0_in, X0_LOADS * (s + 1))
                if not first(s):
                    act.wait_ge(squares_used, s)
                act.activation(squares[:], x0x4[:], ACT.Square).then_inc(squared, 1)

            def place_x0(s):
                act.wait_ge(x0_in, X0_LOADS * (s + 1))
                if not first(s):
                    act.wait_ge(products, layer1_end(s - 1))
                act.activation(x1_ps[:].rearrange("p h c -> p (h c)"), x0x4[:], ACT.Copy).then_inc(x0_placed, 1)

            def finish(s, l, ps, x=None, x_sb=None):
                if x is not None:
                    for to, done in ((x, spread_done[l]), (x_sb, copied[l])):
                        for h in range(2):
                            for copy in range(2):
                                act.activation(to[MAPS * copy:MAPS * (copy + 1), h, :],
                                               ps[MAPS * h:MAPS * (h + 1), :], ACT.Relu).then_inc(done, 1)
                if not first(s):
                    act.wait_ge(summed[l], s)
                act.activation(relu[:, l, :], ps[:], ACT.Relu).then_inc(relu_done[l], 1)

            def mlp(jobs):
                for n in jobs:
                    layer, c, j = MLP[n]
                    act.wait_ge(mlp_mm, n + 1)
                    ps = mlp_ps[n % MLP_BANKS]
                    if layer == 1:
                        act.activation(h1[:, j, :], ps, ACT.Relu, bias=bt1_sb[:, j:j + 1]).then_inc(mlp_act, 1)
                    elif layer == 2:
                        act.activation(h2[:, j, :], ps, ACT.Relu, bias=bt2_sb[:, j:j + 1]).then_inc(mlp_act, 1)
                    else:
                        act.activation(y_sb[:, HALF * c:HALF * (c + 1)], ps[0:1, :], ACT.Copy).then_inc(mlp_act, 1)

            def step(s, turn=None, n=None, last=False):
                if isinstance(s, int) and s <= LATE:
                    copy_shifts(s + 1)
                if turn is not None and not late(s):
                    high(s + 2, turn, n)
                if not last:
                    square(s + 1)
                    place_x0(s + 1)
                act.wait_ge(products_used, layer1_end(s))
                finish(s, 1, y1_ps, x2_ps, x2_sb)
                if not last:
                    act.wait_ge(products_used, layer0_end(s + 1))
                    if turn is not None and not late(s):
                        copy_shifts(s + 2, slice(0, SHIFTS_EARLY))
                    finish(s + 1, 0, y0_ps, x1_ps, x1_sb)
                if late(s):
                    high(s + 2, turn, n)
                elif turn is not None:
                    copy_shifts(s + 2, slice(SHIFTS_EARLY, None))
                if last:
                    mlp(range(MLP_EARLY))
                act.wait_ge(products_used, layer2_end(s, last))
                finish(s, 2, y2_ps)

            high(0, 0, 1)
            copy_shifts(0, slice(0, BANKS // 2))
            place_x0(0)
            square(0)
            copy_shifts(0, slice(BANKS // 2, None))
            act.wait_ge(products_used, layer0_end(0))
            finish(0, 0, y0_ps, x1_ps, x1_sb)
            high(1, 1, 1)
            for s in range(LATE + 2):
                step(s, s % 2, s // 2 + 2)
            with act.Fori(LATE // 2 + 1, STEPS // 2 - 1) as i:
                step(i * 2, 0, i + 2)
                step(i * 2 + 1, 1, i + 2)
            step(STEPS - 2)
            step(STEPS - 1, last=True)
            mlp(range(MLP_EARLY, len(MLP)))

        @block.tensor
        def _(pe):
            def contract(ps, w, moving, first, final):
                for h in range(2):
                    last = pe.matmul(ps[MAPS * h:MAPS * (h + 1), :], w, moving[:, HALF * h:HALF * (h + 1)],
                                     start=first, stop=final)
                return last

            def shift(s, k):
                if k == 0:
                    pe.wait_ge(x0hl_in, 16 * (s + 1))
                if not first(s):
                    pe.wait_ge(shift_copied, BANKS * s + k)
                elif k >= FIRST_BANKS:
                    pe.wait_ge(shift_copied, k - FIRST_BANKS + 1)
                pe.matmul(shift_bank(s, k), shifts_sb[:, k // 2, :], x0hl[:, HALF * (k % 2):HALF * (k % 2 + 1)],
                          start=True, stop=True).then_inc(shifted, 1)

            def groups(end, slot, tiles, ps, w, start, pool_end=None, pool_tiles=(), shifts_of=None, shift_at=()):
                for g, group in enumerate(tiles):
                    k = g - POOL_BEFORE
                    if 0 <= k < len(pool_tiles):
                        pe.wait_ge(pool_products, pool_end - len(pool_tiles) + k + 1)
                        contract(ps, w[:, pool_tiles[k], :], pool_prod[:, k, :], False,
                                 False).then_inc(pool_products_used, 1)
                    pe.wait_ge(products, end - len(tiles) + g + 1)
                    for t in group:
                        if shifts_of is not None and t in shift_at:
                            shift(shifts_of, shift_at.index(t))
                        last = contract(ps, w[:, t, :], prod[:, (slot + g) % RING, t - group[0], :],
                                        start and t == 0, g == len(tiles) - 1 and t == group[-1])
                    last.then_inc(products_used, 1)

            def layer0(s):
                if not first(s):
                    pe.wait_ge(relu_done[0], s)
                pe.wait_ge(squared, s + 1)
                contract(y0_ps, wsq_sb[:], squares[:], True, False).then_inc(squares_used, 1)
                groups(layer0_end(s), slot0(s), SHIFT_RANGES, y0_ps, w0s_sb, False)

            def layer(s, l, ps, w, slot, end, shifts_of=None):
                if not first(s):
                    pe.wait_ge(relu_done[l], s)
                groups(end, slot, GROUP_TILES[l], ps, w, True, pool_end(s, l), POOL_RANGES[l], shifts_of,
                       FIRST_SHIFT_AT[0 if first(s) else 1] if l == 1 else SHIFT_AT)

            def mlp(jobs):
                for n in jobs:
                    layer, c, j = MLP[n]
                    ps = mlp_ps[n % MLP_BANKS]
                    if n >= MLP_BANKS:
                        pe.wait_ge(mlp_act, n - MLP_BANKS + 1)
                    if layer == 1:
                        b = slice(HALF * c, HALF * (c + 1))
                        out_f = slice(P * j, P * (j + 1))
                        pe.wait_ge(zt_ready, 6 * (c + 1))
                        pe.matmul(ps, wt1a_sb[:, out_f], zt_a[:, b], start=True, stop=False)
                        pe.matmul(ps, wt1b_sb[:, out_f], zt_b[:, b], start=False, stop=True).then_inc(mlp_mm, 1)
                        continue
                    pe.wait_ge(mlp_act, max(i for i in range(n) if MLP[i][:2] == (layer - 1, c)) + 1)
                    w, x, ks, rows = ((wt2_sb[:, :, P * j:P * (j + 1)], h1, HID1 // P, P) if layer == 2 else
                                      (wt3_sb[:].unsqueeze(2), h2, HID2 // P, 1))
                    for k in range(ks):
                        last = pe.matmul(ps[0:rows, :], w[:, k, :], x[:, k, :], start=k == 0, stop=k == ks - 1)
                    last.then_inc(mlp_mm, 1)

            def step(s, more=True, last=False):
                layer(s, 1, y1_ps, w1_sb, SLOT1, layer1_end(s), s + 1 if isinstance(s, int) and s <= LATE else None)
                if last:
                    pe.wait_ge(mlp_in, 16 * 7)
                    pe.wait_ge(relu_done[0], STEPS)
                    mlp(range(MLP_EARLY))
                else:
                    layer0(s + 1)
                layer(s, 2, y2_ps, w2_sb, slot2(last), layer2_end(s, last),
                      s + 2 if more and not late(s) else None)

            pe.wait_ge(w0_ready, 4)
            pe.wait_ge(weights_in, 16 * 6)
            for k in range(BANKS):
                shift(0, k)
            layer0(0)
            for s in range(LATE + 1):
                step(s)
            with pe.Fori(LATE + 1, STEPS - 2) as s:
                step(s)
            step(STEPS - 2, more=False)
            step(STEPS - 1, more=False, last=True)

            mlp(range(MLP_EARLY, len(MLP)))


def kernel(**inputs):
    import numpy as np
    import concourse.bacc as bacc
    from concourse.bass_utils import run_bass_kernel_spmd

    get = {k: np.asarray(v) for k, v in inputs.items()}
    w0 = get["L0_rec_W0"]
    m = np.arange(FIELDS)
    shifts = np.array(SHIFTS).T[:, None, :]
    base = np.concatenate([0 * shifts, shifts[:, :, 0:1]], axis=2)
    one = (m[None, :, None] + base) % FIELDS
    other = (one + np.array(DISTANCES).T[:, None, :]) % FIELDS
    moved = (m[None, :, None] + shifts) % FIELDS
    pick = moved.reshape(P, SHIFT_TILES).T[None] == m[:, None, None]
    offsets = np.concatenate([[0], np.cumsum(ROWS)[:-1]]).astype(np.int32)

    def rows_of(w):
        return w.reshape(TILES, P, MAPS).transpose(1, 0, 2)

    arrays = {
        "table": np.concatenate([get[f"tbl_{f}"] for f in range(FIELDS)], axis=0),
        "ids": get["ids"].T.reshape(FIELDS, STEPS, QUART, GATHERS).transpose(0, 2, 1, 3).reshape(P, -1),
        "id_offset": np.repeat(offsets, QUART)[:, None].repeat(GATHERS, axis=1),
        "dense_t": get["dense_ctx"].T,
        "w0_a": w0[one, other].reshape(P, PAIR_TILES, MAPS),
        "w0_b": w0[other, one].reshape(P, PAIR_TILES, MAPS),
        "w0_sq": np.tile(w0[m, m], (QUART, 1)),
        "w1": rows_of(get["L0_rec_W1"]),
        "w2": rows_of(get["L0_rec_W2"]),
        "shifts": np.tile(pick.astype(np.float32), (2, 1, 1)),
        "wt1_a": get["W_top1"][0:P],
        "wt1_b": get["W_top1"][P:],
        "bt1": get["b_top1"].reshape(HID1 // P, P).T,
        "wt2": get["W_top2"].reshape(HID1 // P, P, HID2).transpose(1, 0, 2),
        "bt2": get["b_top2"].reshape(HID2 // P, P).T,
        "wt3": get["W_top3"].reshape(HID2 // P, P).T,
    }
    arrays = {k: np.ascontiguousarray(a) for k, a in arrays.items()}
    nc = bacc.Bacc("TRN2", target_bir_lowering=False, num_devices=1)
    args = [nc.dram_tensor(k, a.shape, mybir.dt.from_np(a.dtype), kind="ExternalInput").ap()
            for k, a in arrays.items()]
    x0_rows = nc.dram_tensor("x0_rows", [FIELDS, COLS], F32, kind="Internal").ap()
    x0_parts = nc.dram_tensor("x0_parts", [2 * FIELDS, COLS], F32, kind="Internal").ap()
    out = nc.dram_tensor("out", [BATCH, 1], F32, kind="ExternalOutput").ap()
    cin_tower_kernel(nc, *args, x0_rows, x0_parts, out)
    r = run_bass_kernel_spmd(nc, [arrays], core_ids=[0])
    return r.results[0]["out"]
```
